# Optimizing a Trainium2 kernel written in Bass

```python
import numpy as np
import jax
import jax.numpy as jnp

def _softmax(x, axis=-1):
    return jax.nn.softmax(x, axis=axis)

def _gelu(x):
    return jax.nn.gelu(x, approximate=True)

def _silu(x):
    return jax.nn.silu(x)

def _sigmoid(x):
    return jax.nn.sigmoid(x)

def _layernorm(x, axis=-1, eps=1e-05):
    m = jnp.mean(x, axis=axis, keepdims=True)
    v = jnp.var(x, axis=axis, keepdims=True)
    return (x - m) / jnp.sqrt(v + eps)

def _scatter_add(tgt, idx, src, axis=0):
    return tgt.at[idx].add(src)

def _segment_sum(src, seg, n):
    return jax.ops.segment_sum(src, seg, n)
kernel_name = 'mk_hybrid_d1_jaxref_r4_df23ad'

def setup_inputs(seed: int=0):
    np.random.seed(seed)
    _w = jnp.asarray

    def _L0_attn_a_setup():
        import jax, jax.numpy as jnp
        import numpy as np
        B, N, D, H, DH = (2, 512, 256, 16, 64)
        key = jax.random.key(seed)
        ks = jax.random.split(key, 5)
        x = jax.random.normal(ks[0], (B, N, D), dtype=jnp.float32)
        Wq = jax.random.normal(ks[1], (D, H * DH), dtype=jnp.float32) * 0.02
        Wk = jax.random.normal(ks[2], (D, H * DH), dtype=jnp.float32) * 0.02
        Wv = jax.random.normal(ks[3], (D, H * DH), dtype=jnp.float32) * 0.02
        Wo = jax.random.normal(ks[4], (H * DH, D), dtype=jnp.float32) * 0.02
        bo = jnp.zeros((D,), dtype=jnp.float32)
        return {'x': x, 'Wq': Wq, 'Wk': Wk, 'Wv': Wv, 'Wo': Wo, 'bo': bo}
    _L0_attn_a_in = _L0_attn_a_setup()

    def _L0_attn_b_setup():
        import jax, jax.numpy as jnp
        import numpy as np
        EPS = 1e-05

        def exp_map_at_origin(v, c):
            sqrt_c = jnp.sqrt(c)
            v_norm = jnp.maximum(jnp.linalg.norm(v, axis=-1, keepdims=True), EPS)
            return 1.0 / sqrt_c * jnp.tanh(sqrt_c * v_norm) * (v / v_norm)

        def log_map_at_origin(y, c):
            sqrt_c = jnp.sqrt(c)
            y_norm = jnp.maximum(jnp.linalg.norm(y, axis=-1, keepdims=True), EPS)
            y_norm_clamped = jnp.minimum(y_norm, 1.0 / sqrt_c - EPS)
            return 1.0 / sqrt_c * jnp.arctanh(sqrt_c * y_norm_clamped) * (y / y_norm)

        def poincare_distance(x, y, c):
            sqrt_c = jnp.sqrt(c)
            xns = jnp.sum(x * x, axis=-1, keepdims=True)
            yns = jnp.sum(y * y, axis=-1, keepdims=True)
            xy = jnp.einsum('bhsd,bhtd->bhst', x, y)
            xnsb = xns
            ynsb = jnp.swapaxes(yns, -2, -1)
            diff_norm_sq = xnsb - 2.0 * xy + ynsb
            denom = jnp.maximum((1.0 - c * xnsb) * (1.0 - c * ynsb), EPS)
            arg = jnp.maximum(1.0 + 2.0 * c * diff_norm_sq / denom, 1.0 + EPS)
            return 1.0 / sqrt_c * jnp.arccosh(arg)
        key = jax.random.key(seed)
        ks = jax.random.split(key, 5)
        B, S, D = (2, 256, 256)
        x = jax.random.normal(ks[0], (B, S, D), dtype=jnp.float32)
        scale = 0.02
        W_q = scale * jax.random.normal(ks[1], (D, D), dtype=jnp.float32)
        W_k = scale * jax.random.normal(ks[2], (D, D), dtype=jnp.float32)
        W_v = scale * jax.random.normal(ks[3], (D, D), dtype=jnp.float32)
        W_o = scale * jax.random.normal(ks[4], (D, D), dtype=jnp.float32)
        return {'x': x, 'W_q': W_q, 'W_k': W_k, 'W_v': W_v, 'W_o': W_o, 'log_c': jnp.zeros((), jnp.float32), 'beta': jnp.zeros((), jnp.float32), 'attention_bias': jnp.zeros((), jnp.float32)}
    _L0_attn_b_in = _L0_attn_b_setup()

    def _L0_ffn_setup():
        import jax, jax.numpy as jnp
        import numpy as np
        B, S, D, O, E, R = (8, 512, 256, 256, 8, 4)
        TOP_K = 2
        SCALING = 4.0 / 4.0
        key = jax.random.key(seed)
        k0, k1, k2, k3, k4 = jax.random.split(key, 5)
        hidden_states = jax.random.normal(k0, (B, S, D), dtype=jnp.float32)
        W_lin = jax.random.normal(k1, (O, D), dtype=jnp.float32) * 0.02
        b_lin = jnp.zeros((O,), dtype=jnp.float32)
        gate_w = jax.random.normal(k2, (E, D), dtype=jnp.float32) * 0.02
        left = jax.random.normal(k3, (E, D, R), dtype=jnp.float32) * 0.02
        right = jax.random.normal(k4, (E, R, O), dtype=jnp.float32) * 0.02
        return {'hidden_states': hidden_states, 'W_lin': W_lin, 'b_lin': b_lin, 'gate_w': gate_w, 'left': left, 'right': right}
    _L0_ffn_in = _L0_ffn_setup()
    _d = {'L0_attn_a_x': _L0_attn_a_in['x'], 'L0_attn_a_Wq': _L0_attn_a_in['Wq'], 'L0_attn_a_Wk': _L0_attn_a_in['Wk'], 'L0_attn_a_Wv': _L0_attn_a_in['Wv'], 'L0_attn_a_Wo': _L0_attn_a_in['Wo'], 'L0_attn_a_bo': _L0_attn_a_in['bo'], 'L0_attn_b_W_q': _L0_attn_b_in['W_q'], 'L0_attn_b_W_k': _L0_attn_b_in['W_k'], 'L0_attn_b_W_v': _L0_attn_b_in['W_v'], 'L0_attn_b_W_o': _L0_attn_b_in['W_o'], 'L0_attn_b_log_c': _L0_attn_b_in['log_c'], 'L0_attn_b_beta': _L0_attn_b_in['beta'], 'L0_attn_b_attention_bias': _L0_attn_b_in['attention_bias'], 'L0_ffn_W_lin': _L0_ffn_in['W_lin'], 'L0_ffn_b_lin': _L0_ffn_in['b_lin'], 'L0_ffn_gate_w': _L0_ffn_in['gate_w'], 'L0_ffn_left': _L0_ffn_in['left'], 'L0_ffn_right': _L0_ffn_in['right']}
    _x0 = _d['L0_attn_a_x']
    _d['L0_attn_a_x'] = jax.random.normal(jax.random.fold_in(jax.random.key(seed), 1), (2, 2048, 256), dtype=_x0.dtype)
    del _x0
    return _d

def reference(L0_attn_a_x, L0_attn_a_Wq, L0_attn_a_Wk, L0_attn_a_Wv, L0_attn_a_Wo, L0_attn_a_bo, L0_attn_b_W_q, L0_attn_b_W_k, L0_attn_b_W_v, L0_attn_b_W_o, L0_attn_b_log_c, L0_attn_b_beta, L0_attn_b_attention_bias, L0_ffn_W_lin, L0_ffn_b_lin, L0_ffn_gate_w, L0_ffn_left, L0_ffn_right):

    def _L0_attn_a_ref(x, Wq, Wk, Wv, Wo, bo):
        import jax, jax.numpy as jnp
        import numpy as np
        B, N, D, H, DH = (2, 512, 256, 16, 64)
        b, n, _ = x.shape
        scale = DH ** (-0.5)
        q = (x @ Wq).reshape(b, n, H, DH)
        k = (x @ Wk).reshape(b, n, H, DH)
        v = (x @ Wv).reshape(b, n, H, DH)
        base = (2.0 ** 8) ** (1.0 / H)
        slope = 1.0 / base ** jnp.arange(1, H + 1, dtype=jnp.float32)
        pos = jnp.arange(n, dtype=jnp.float32)
        bias = slope[:, None, None] * (pos[:, None] - pos[None, :])
        scores = jnp.einsum('bihd,bjhd->bhij', q, k) * scale + bias[None]
        causal = pos[:, None] >= pos[None, :]
        scores = jnp.where(causal[None, None], scores, jnp.float32(-1e+30))
        attn = jax.nn.softmax(scores, axis=-1)
        out = jnp.einsum('bhij,bjhd->bihd', attn, v).reshape(b, n, H * DH)
        return out @ Wo + bo

    def _L0_attn_b_ref(x, W_q, W_k, W_v, W_o, log_c, beta, attention_bias):
        import jax, jax.numpy as jnp
        import numpy as np
        EPS = 1e-05

        def exp_map_at_origin(v, c):
            sqrt_c = jnp.sqrt(c)
            v_norm = jnp.maximum(jnp.linalg.norm(v, axis=-1, keepdims=True), EPS)
            return 1.0 / sqrt_c * jnp.tanh(sqrt_c * v_norm) * (v / v_norm)

        def log_map_at_origin(y, c):
            sqrt_c = jnp.sqrt(c)
            y_norm = jnp.maximum(jnp.linalg.norm(y, axis=-1, keepdims=True), EPS)
            y_norm_clamped = jnp.minimum(y_norm, 1.0 / sqrt_c - EPS)
            return 1.0 / sqrt_c * jnp.arctanh(sqrt_c * y_norm_clamped) * (y / y_norm)

        def poincare_distance(x, y, c):
            sqrt_c = jnp.sqrt(c)
            xns = jnp.sum(x * x, axis=-1, keepdims=True)
            yns = jnp.sum(y * y, axis=-1, keepdims=True)
            xy = jnp.einsum('bhsd,bhtd->bhst', x, y)
            xnsb = xns
            ynsb = jnp.swapaxes(yns, -2, -1)
            diff_norm_sq = xnsb - 2.0 * xy + ynsb
            denom = jnp.maximum((1.0 - c * xnsb) * (1.0 - c * ynsb), EPS)
            arg = jnp.maximum(1.0 + 2.0 * c * diff_norm_sq / denom, 1.0 + EPS)
            return 1.0 / sqrt_c * jnp.arccosh(arg)
        B, S, D = x.shape
        H = 16
        dh = D // H
        c = jax.nn.softplus(log_c)
        beta_pos = jax.nn.softplus(beta)

        def split_heads(t):
            return jnp.transpose(t.reshape(B, S, H, dh), (0, 2, 1, 3))
        q_t = split_heads(x @ W_q.T)
        k_t = split_heads(x @ W_k.T)
        v_t = split_heads(x @ W_v.T)
        q_h = exp_map_at_origin(q_t, c)
        k_h = exp_map_at_origin(k_t, c)
        v_h = exp_map_at_origin(v_t, c)
        dist = poincare_distance(q_h, k_h, c)
        scores = -beta_pos * dist - attention_bias
        weights = jax.nn.softmax(scores, axis=-1)
        v_tan = log_map_at_origin(v_h, c)
        out_tan = jnp.einsum('bhst,bhtd->bhsd', weights, v_tan)
        out_hyp = exp_map_at_origin(out_tan, c)
        out_heads_tan = log_map_at_origin(out_hyp, c)
        concat = jnp.transpose(out_heads_tan, (0, 2, 1, 3)).reshape(B, S, D)
        return concat @ W_o.T

    def _L0_ffn_ref(hidden_states, W_lin, b_lin, gate_w, left, right):
        import jax, jax.numpy as jnp
        import numpy as np
        B, S, D, O, E, R = (8, 512, 256, 256, 8, 4)
        TOP_K = 2
        SCALING = 4.0 / 4.0
        bsz, seq, d_in = hidden_states.shape
        x = hidden_states.reshape(-1, d_in)
        logits = x @ gate_w.T
        scores = jax.nn.softmax(logits, axis=-1)
        weights, idx = jax.lax.top_k(scores, TOP_K)
        base = x @ W_lin.T + b_lin
        left_sel = left[idx]
        right_sel = right[idx]
        t = jnp.einsum('nd,nkdr->nkr', x, left_sel)
        out_k = jnp.einsum('nkr,nkro->nko', t, right_sel)
        lora = jnp.sum(weights[..., None] * out_k, axis=1) * SCALING
        return (base + lora).reshape(bsz, seq, -1)
    x = L0_attn_a_x
    x = x + _L0_attn_a_ref(_layernorm(x, axis=-1), L0_attn_a_Wq, L0_attn_a_Wk, L0_attn_a_Wv, L0_attn_a_Wo, L0_attn_a_bo)
    x = x + _L0_ffn_ref(_layernorm(x, axis=-1), L0_ffn_W_lin, L0_ffn_b_lin, L0_ffn_gate_w, L0_ffn_left, L0_ffn_right)
    x = x + _L0_attn_b_ref(_layernorm(x, axis=-1), L0_attn_b_W_q, L0_attn_b_W_k, L0_attn_b_W_v, L0_attn_b_W_o, L0_attn_b_log_c, L0_attn_b_beta, L0_attn_b_attention_bias)
    x = x + _L0_ffn_ref(_layernorm(x, axis=-1), L0_ffn_W_lin, L0_ffn_b_lin, L0_ffn_gate_w, L0_ffn_left, L0_ffn_right)
    return x

_drawn_inputs = setup_inputs


def setup_inputs(seed=0):
    import zlib

    import numpy as np

    out = dict(_drawn_inputs(seed))
    spreads = {'L0_attn_a_bo': (0.0, 0.1), 'L0_ffn_b_lin': (0.0, 0.1)}
    factors = {'L0_attn_a_Wq': 8.0,
     'L0_attn_a_Wk': 8.0,
     'L0_attn_b_W_q': 8.0,
     'L0_attn_b_W_k': 8.0,
     'L0_attn_b_W_v': 4.828,
     'L0_attn_b_W_o': 4.472,
     'L0_ffn_gate_w': 8.0,
     'L0_ffn_left': 8.0,
     'L0_ffn_right': 8.0}
    for name, (base, spread) in spreads.items():
        noise = np.random.default_rng([zlib.crc32(name.encode()), seed]).standard_normal(out[name].shape)
        drawn = base * np.exp(spread * noise) if base else spread * noise
        out[name] = jnp.asarray(drawn.astype(out[name].dtype))
    for name, factor in factors.items():
        out[name] = (out[name] * factor).astype(out[name].dtype)
    return out
```

```python
from contextlib import ExitStack

import concourse.bass as bass
from concourse import mybir

F32 = mybir.dt.float32
F32R = mybir.dt.float32r
BF16 = mybir.dt.bfloat16
U32 = mybir.dt.uint32
ALU = mybir.AluOpType
ACT = mybir.ActivationFunctionType
AX = mybir.AxisListType

P = 128
BATCH, SEQ, D = 2, 2048, 256
TB = SEQ // P
NT = BATCH * TB
KC = D // P
LN_EPS = 1e-5
BANK = 512


class Env:
    pass


def make_env(nc, ctx):
    e = Env()
    e.ctx = ctx
    e.X = ctx.enter_context(nc.sbuf_tensor("X", [P, NT, D], F32))
    e.ident = ctx.enter_context(nc.sbuf_tensor("ident", [P, P], F32))
    e.ident_bf = ctx.enter_context(nc.sbuf_tensor("ident_bf", [P, P], BF16))
    e.mean = ctx.enter_context(nc.sbuf_tensor("ln_mean", [P, NT], F32))
    e.rstd = ctx.enter_context(nc.sbuf_tensor("ln_rstd", [P, NT], F32))
    e.ln_eps = ctx.enter_context(nc.sbuf_tensor("ln_eps", [P, 1], F32))
    e.psum = ctx.enter_context(nc.psum_tensor("psum", [P, 8 * BANK], F32))
    return e


def stage_load(nc, env, x):
    with ExitStack() as ctx:
        x_loaded = env.ctx.enter_context(nc.semaphore("x_loaded"))
        consts = env.ctx.enter_context(nc.semaphore("consts"))
        block = ctx.enter_context(nc.Block())
        xv = x.rearrange("(t p) d -> p t d", p=P)

        @block.sync
        def _(sp):
            for q in range(4):
                sl = slice(q * NT // 4, (q + 1) * NT // 4)
                sp.dma_start(env.X[:, sl, :], xv[:, sl, :]).then_inc(x_loaded, 16)
            sp.wait_ge(x_loaded, 64)

        @block.gpsimd
        def _(pool):
            pool.memset(env.ident[:, :], 0.0).then_inc(consts, 1)
            pool.memset(env.ident_bf[:, :], 0.0).then_inc(consts, 1)
            pool.memset(env.ln_eps[:, :], LN_EPS).then_inc(consts, 1)
            pool.wait_ge(consts, 3)
            for m in (env.ident, env.ident_bf):
                pool.affine_select(out=m[:, :], in_=m[:, :], compare_op=ALU.not_equal, fill=1.0, base=0,
                                   pattern=[[-1, P]], channel_multiplier=1).then_inc(consts, 1)
            pool.wait_ge(consts, 5)


def stage_ln_stats(nc, env, name):
    with ExitStack() as ctx:
        stats = ctx.enter_context(nc.sbuf_tensor(f"{name}_stats", [P, NT, 6], F32))
        tmp = ctx.enter_context(nc.sbuf_tensor(f"{name}_tmp", [P, 4, NT], F32))
        stats_done = env.ctx.enter_context(nc.semaphore(f"{name}_stats_done"))
        step = env.ctx.enter_context(nc.semaphore(f"{name}_step"))
        var_done = env.ctx.enter_context(nc.semaphore(f"{name}_var_done"))
        std_done = env.ctx.enter_context(nc.semaphore(f"{name}_std_done"))
        block = ctx.enter_context(nc.Block())

        @block.vector
        def _(dve):
            with dve.Fori(0, NT) as t:
                nc.vector.bn_stats(stats[:, bass.ds(t, 1), :].rearrange("p a s -> p (a s)"),
                                   env.X[:, bass.ds(t, 1), :].rearrange("p a d -> p (a d)")).then_inc(stats_done, 1)
            dve.wait_ge(stats_done, NT)
            m0, v0, m1, v1 = (stats[:, :, i] for i in (1, 2, 4, 5))
            nc.vector.tensor_tensor(tmp[:, 0, :], m0, m1, ALU.add).then_inc(step, 1)
            nc.vector.tensor_tensor(tmp[:, 1, :], m0, m1, ALU.subtract).then_inc(step, 1)
            nc.vector.tensor_tensor(tmp[:, 2, :], v0, v1, ALU.add).then_inc(step, 1)
            dve.wait_ge(step, 3)
            nc.vector.tensor_scalar(env.mean[:, :], tmp[:, 0, :], 0.5, None, ALU.mult).then_inc(step, 1)
            nc.vector.tensor_tensor(tmp[:, 3, :], tmp[:, 1, :], tmp[:, 1, :], ALU.mult).then_inc(step, 1)
            dve.wait_ge(step, 5)
            nc.vector.tensor_scalar(tmp[:, 3, :], tmp[:, 3, :], D / 4.0, None, ALU.mult).then_inc(step, 1)
            dve.wait_ge(step, 6)
            nc.vector.tensor_tensor(tmp[:, 0, :], tmp[:, 2, :], tmp[:, 3, :], ALU.add).then_inc(var_done, 1)
            dve.wait_ge(std_done, 1)
            nc.vector.reciprocal(env.rstd[:, :], tmp[:, 1, :]).then_inc(step, 1)
            dve.wait_ge(step, 7)

        @block.scalar
        def _(act):
            act.wait_ge(var_done, 1)
            nc.scalar.activation(tmp[:, 1, :], tmp[:, 0, :], ACT.Sqrt, bias=env.ln_eps[:, 0:1],
                                 scale=1.0 / D).then_inc(std_done, 1)


E, R = 8, 4
NB_OUT = D + E + E * R


def stage_ffn(nc, env, name, w_cat, right_aug, out=None):
    RA = E * R + 1
    with ExitStack() as ctx:
        def sb(n, shape, dt=F32):
            return ctx.enter_context(nc.sbuf_tensor(f"{name}_{n}", shape, dt))

        def sem(n):
            return env.ctx.enter_context(nc.semaphore(f"{name}_{n}"))

        wc = sb("wc", [P, KC, NB_OUT])
        ra = sb("ra", [RA, D])
        iota = sb("iota", [P, E])
        xn = sb("xn", [P, 2, D])
        xnT = sb("xnT", [P, 2, D])
        prob = sb("prob", [P, 2, E])
        nmax = sb("nmax", [P, 2])
        zsum = sb("zsum", [P, 2])
        zinv = sb("zinv", [P, 2])
        top = sb("top", [P, 2, 8])
        idx = sb("idx", [P, 2, 8], U32)
        idxf = sb("idxf", [P, 2, 2])
        wgt = sb("wgt", [P, 2, 3, E])
        tl = sb("tl", [P, 2, RA])
        tlT = sb("tlT", [RA, 2, P])
        w_loaded, iota_done, ones_done = sem("w_loaded"), sem("iota_done"), sem("ones_done")
        xn_done, xT_done, xT_copied = sem("xn_done"), sem("xT_done"), sem("xT_copied")
        joint_done, max_done, exp_done = sem("joint_done"), sem("max_done"), sem("exp_done")
        chain, tl_done, tlT_done, tlT_copied = sem("chain"), sem("tl_done"), sem("tlT_done"), sem("tlT_copied")
        lora_done, x_added, stored = sem("lora_done"), sem("x_added"), sem("stored")
        passed = sem("passed")
        block = ctx.enter_context(nc.Block())

        def ps_xT(j):
            return env.psum[:, j * BANK:j * BANK + D]

        def ps_joint(j, a, b):
            return env.psum[:, (2 + j) * BANK + a:(2 + j) * BANK + b]

        def ps_tlT(j):
            return env.psum[0:RA, (4 + j) * BANK:(4 + j) * BANK + P]

        def tile_of_X(t):
            return env.X[:, bass.ds(t, 1), :].rearrange("p a d -> p (a d)")

        @block.sync
        def _(sp):
            sp.dma_start(wc[:, :, :], w_cat.rearrange("(c p) n -> p c n", p=P)).then_inc(w_loaded, 16)
            sp.dma_start(ra[:, :], right_aug).then_inc(w_loaded, 16)
            if out is not None:
                ov = out.rearrange("(t p) d -> p t d", p=P)
                for q in range(8):
                    n = NT // 8
                    sp.wait_ge(x_added, (q + 1) * n)
                    sp.dma_start(ov[:, q * n:(q + 1) * n, :], env.X[:, q * n:(q + 1) * n, :]).then_inc(stored, 16)
                sp.wait_ge(stored, 16 * 8)

        @block.gpsimd
        def _(pool):
            for j in range(E):
                pool.memset(iota[:, j:j + 1], float(j)).then_inc(iota_done, 1)
            for j in range(2):
                pool.memset(tl[:, j, E * R:RA], 1.0).then_inc(ones_done, 1)

        @block.vector
        def _(dve):
            n_chain = [0]

            def link(ins, per_iter, i, k):
                ins.then_inc(chain, 1)
                dve.wait_ge(chain, i * per_iter + k)
                dve.sem_inc(passed, 1)

            def normalize(t, j, first=False):
                if not first:
                    dve.wait_ge(xT_done, t - 1)
                nc.vector.tensor_scalar(xn[:, j, :], tile_of_X(t), env.mean[:, bass.ds(t, 1)],
                                        env.rstd[:, bass.ds(t, 1)], ALU.subtract, ALU.mult).then_inc(xn_done, 1)

            STEPS = 7
            dve.wait_ge(iota_done, E)
            dve.wait_ge(ones_done, 2)

            def route(t, j):
                dve.wait_ge(joint_done, t + 1)
                nc.vector.reduce_max(nmax[:, j:j + 1], ps_joint(j, D, D + E), AX.X, negate=True).then_inc(max_done, 1)
                dve.wait_ge(exp_done, t + 1)
                link(nc.vector.reciprocal(zinv[:, j:j + 1], zsum[:, j:j + 1]), STEPS, t, 1)
                link(nc.vector.tensor_scalar(prob[:, j, :], prob[:, j, :], zinv[:, j:j + 1], None, ALU.mult), STEPS, t, 2)
                link(nc.vector.max(top[:, j, :], prob[:, j, :]), STEPS, t, 3)
                link(nc.vector.max_index(idx[:, j, :], top[:, j, :], prob[:, j, :]), STEPS, t, 4)
                link(nc.vector.tensor_copy(idxf[:, j, :], idx[:, j, 0:2]), STEPS, t, 5)
                nc.vector.tensor_scalar(wgt[:, j, 0, :], iota[:, :], idxf[:, j, 0:1], top[:, j, 0:1],
                                        ALU.is_equal, ALU.mult)
                link(nc.vector.tensor_scalar(wgt[:, j, 1, :], iota[:, :], idxf[:, j, 1:2], top[:, j, 1:2],
                                             ALU.is_equal, ALU.mult), STEPS, t, 6)
                link(nc.vector.tensor_tensor(wgt[:, j, 2, :], wgt[:, j, 0, :], wgt[:, j, 1, :], ALU.add), STEPS, t, 7)
                nc.vector.tensor_tensor(tl[:, j, 0:E * R].rearrange("p (e r) -> p e r", r=R),
                                        ps_joint(j, D + E, NB_OUT).rearrange("p (e r) -> p e r", r=R),
                                        wgt[:, j, 2, :].unsqueeze(2).to_broadcast([P, E, R]),
                                        ALU.mult).then_inc(tl_done, 1)

            def add(t, j):
                dve.wait_ge(lora_done, t + 1)
                nc.vector.tensor_tensor(tile_of_X(t), ps_joint(j, 0, D), tile_of_X(t), ALU.add).then_inc(x_added, 1)

            for j in range(2):
                nc.vector.tensor_scalar(xn[:, j, :], env.X[:, j, :], env.mean[:, j:j + 1], env.rstd[:, j:j + 1],
                                        ALU.subtract, ALU.mult).then_inc(xn_done, 1)
            with dve.Fori(0, NT // 2 - 1) as pair:
                t = pair * 2
                for j in range(2):
                    route(t + j, j)
                    normalize(t + j + 2, j)
                for j in range(2):
                    add(t + j, j)
            for j in range(2):
                route(NT - 2 + j, j)
            for j in range(2):
                dve.wait_ge(lora_done, NT - 1 + j)
                nc.vector.tensor_tensor(env.X[:, NT - 2 + j, :], ps_joint(j, 0, D), env.X[:, NT - 2 + j, :],
                                        ALU.add).then_inc(x_added, 1)
            dve.wait_ge(x_added, NT)

        @block.scalar
        def _(act):
            def transposed(t, j):
                act.wait_ge(xT_done, t + 1)
                nc.scalar.activation(xnT[:, j, :], ps_xT(j), ACT.Copy).then_inc(xT_copied, 1)

            def exps(t, j):
                act.wait_ge(max_done, t + 1)
                nc.scalar.activation(prob[:, j, :], ps_joint(j, D, D + E), ACT.Exp, bias=nmax[:, j:j + 1],
                                     accum_out=zsum[:, j:j + 1]).then_inc(exp_done, 1)

            def weighted(t, j):
                act.wait_ge(tlT_done, t + 1)
                nc.scalar.activation(tlT[:, j, :], ps_tlT(j), ACT.Copy).then_inc(tlT_copied, 1)

            nc.scalar.preload_act_table_set("exp_and_others")
            with act.Fori(0, NT // 2) as pair:
                t = pair * 2
                for j in range(2):
                    transposed(t + j, j)
                for j in range(2):
                    exps(t + j, j)
                for j in range(2):
                    weighted(t + j, j)

        @block.tensor
        def _(pe):
            pe.wait_ge(w_loaded, 32)

            def transpose_x(t, j):
                pe.wait_ge(xn_done, t + 1)
                for c in range(KC):
                    last = nc.tensor.transpose(ps_xT(j)[:, c * P:(c + 1) * P], xn[:, j, c * P:(c + 1) * P], env.ident[:, :])
                last.then_inc(xT_done, 1)

            def joint(t, j, wait_add):
                pe.wait_ge(xT_copied, t + 1)
                if wait_add:
                    pe.wait_ge(x_added, t - 1)
                for c in range(KC):
                    last = nc.tensor.matmul(ps_joint(j, 0, NB_OUT), xnT[:, j, c * P:(c + 1) * P], wc[:, c, :],
                                            start=(c == 0), stop=(c == KC - 1))
                last.then_inc(joint_done, 1)

            def lora(t, j):
                pe.wait_ge(tl_done, t + 1)
                pe.sem_inc(passed, 1)
                nc.tensor.transpose(ps_tlT(j), tl[:, j, :], env.ident[:, :]).then_inc(tlT_done, 1)
                pe.wait_ge(tlT_copied, t + 1)
                nc.tensor.matmul(ps_joint(j, 0, D), tlT[:, j, :], ra[:, :], start=False, stop=True,
                                 skip_group_check=True).then_inc(lora_done, 1)

            for j in range(2):
                transpose_x(j, j)
            for j in range(2):
                joint(j, j, False)
            for j in range(2):
                lora(j, j)
            with pe.Fori(1, NT // 2) as pair:
                t = pair * 2
                for j in range(2):
                    transpose_x(t + j, j)
                for j in range(2):
                    joint(t + j, j, True)
                for j in range(2):
                    lora(t + j, j)


HA, DH = 16, 64
PAIRS = HA // 2
IB = 256
NIB = SEQ // IB
SCALE = DH ** -0.5
NEG = -1e30


def stage_attn_a(nc, env, wqk, wv, wo, bo, slopes):
    UNITS = 2 * TB
    chunks, evacs = [], []
    for u in range(UNITS):
        n = (u // 2 + 1) * P
        chunks.append([(a, min(a + 2 * BANK, n)) for a in range(0, n, 2 * BANK)])
        evacs.append([(a, min(a + 4, u // 2 + 1)) for a in range(0, u // 2 + 1, 4)])
    chunk0 = [sum(len(c) for c in chunks[:u]) for u in range(UNITS + 1)]
    evac0 = [sum(len(c) for c in evacs[:u]) for u in range(UNITS + 1)]
    NCH, NEV = chunk0[UNITS], evac0[UNITS]
    LAG = 2
    ROWS = 3
    NV, NQK = 4, 16
    NPROJ = NV + NQK
    on_dve = [e % 3 == 2 for e in range(NEV)]

    def count(flags, upto):
        return sum(flags[:upto])

    n_dve = count(on_dve, NEV)
    n_act = NEV - n_dve
    av_step = {ib: 4 * (ib + 1) + LAG for ib in range(NIB)}
    op_step = {ib: 4 * (ib + 1) + LAG + 2 for ib in range(NIB)}
    STEPS = UNITS + LAG + 4

    with ExitStack() as ctx:
        def sb(n, shape, dt=F32):
            return ctx.enter_context(nc.sbuf_tensor(f"a_{n}", shape, dt))

        def sem(n):
            return env.ctx.enter_context(nc.semaphore(f"a_{n}"))

        xn = sb("xn", [P, 4, D])
        xnT = sb("xnT", [P, KC, SEQ])
        wqk_sb = sb("wqk", [P, 2, 2, KC, 2, DH])
        wv_sb = sb("wv", [P, KC, 2 * DH])
        wo_sb = sb("wo", [P, D])
        bo_sb = sb("bo", [P, D])
        slope_sb = sb("slope", [P, HA])
        iota_j = sb("iota_j", [P, SEQ])
        bias = sb("bias", [P, 2, SEQ])
        mask = sb("mask", [P, P], BF16)
        q_st = sb("q_st", [P, 2, SEQ], F32R)
        k_hi = sb("k_hi", [P, 2, SEQ], F32R)
        k_lo = sb("k_lo", [P, 2, SEQ], F32R)
        v_sb = sb("v", [P, TB, 2 * DH])
        srow = sb("srow", [P, ROWS, SEQ])
        pT = sb("pT", [P, 2, TB, IB])
        cmax = sb("cmax", [P, UNITS, 2])
        nmax = sb("nmax", [P, UNITS])
        zsum = sb("zsum", [P, UNITS])
        zinv = sb("zinv", [P, UNITS])
        zrep = sb("zrep", [P, 4, 2, DH])
        zT = sb("zT", [P, IB])
        oT = sb("oT", [P, 2, IB])

        consts, w_loaded, wo_loaded, mask_done = sem("consts"), sem("w_loaded"), sem("wo_loaded"), sem("mask_done")
        iota_done = sem("iota_done")
        xn_done, xT_done, xT_copied = sem("xn_done"), sem("xT_done"), sem("xT_copied")
        proj_done, v_copied, hi_done, lo_done = sem("proj_done"), sem("v_copied"), sem("hi_done"), sem("lo_done")
        bias_done = sem("bias_done")
        scores_done, max_done, nmax_done = sem("scores_done"), sem("max_done"), sem("nmax_done")
        exp_done, zinv_done, zrep_done = sem("exp_done"), sem("zinv_done"), sem("zrep_done")
        probT_done, act_evac, dve_evac = sem("probT_done"), sem("act_evac"), sem("dve_evac")
        zT_done, zT_copied, av_done, oT_done = sem("zT_done"), sem("zT_copied"), sem("av_done"), sem("oT_done")
        op_done, x_added = sem("op_done"), sem("x_added")
        passed = sem("passed")
        block = ctx.enter_context(nc.Block())

        PT_BANKS = (4, 5, 7)

        def bank(i, a=0, b=BANK):
            return env.psum[:, i * BANK + a:i * BANK + b]

        def ps_scores(c, width):
            return env.psum[:, (c % 2) * 2 * BANK:(c % 2) * 2 * BANK + width]

        def evacuate(eng, copy, u, g, dve_side):
            h, it = u % 2, u // 2
            il = it % 2
            for i, (a, z) in enumerate(evacs[u]):
                e = evac0[u] + i
                if on_dve[e] != dve_side:
                    continue
                eng.wait_ge(probT_done, g * NEV + e + 1)
                if it % 2 == 0 and i == 0 or (it % 2 == 0 and count(on_dve, e) == count(on_dve, evac0[u]) and dve_side):
                    if it >= 2:
                        eng.wait_ge(av_done, g * NIB + it // 2)
                    else:
                        eng.wait_ge(av_done, g * NIB)
                src = bank(PT_BANKS[e % 3], 0, (z - a) * P).rearrange("p (j i) -> p j i", i=P)
                copy(pT[:, h, a:z, il * P:(il + 1) * P], src).then_inc(dve_evac if dve_side else act_evac, 1)

        @block.sync
        def _(sp):
            sp.dma_start(bo_sb[:, :], bo.to_broadcast([P, D])).then_inc(consts, 16)
            sp.dma_start(slope_sb[:, :], slopes.to_broadcast([P, HA])).then_inc(consts, 16)
            with sp.Fori(0, BATCH) as b:
                with sp.Fori(0, PAIRS) as hp:
                    g = b * PAIRS + hp
                    sp.wait_ge(proj_done, g * NPROJ)
                    for h in range(2):
                        for c in range(2):
                            sp.dma_start(wqk_sb[:, h, :, :, c, :],
                                         wqk[bass.ds(hp * 2 + h, 1)].rearrange("a p t c d -> p (a t) c d")
                                         ).then_inc(w_loaded, 16)
                    sp.dma_start(wv_sb[:, :, :], wv[bass.ds(hp, 1)].rearrange("a p c d -> p (a c) d")).then_inc(w_loaded, 16)
                    sp.wait_ge(op_done, g * NIB)
                    sp.dma_start(wo_sb[:, :], wo[bass.ds(hp, 1)].rearrange("a p d -> p (a d)")).then_inc(wo_loaded, 16)

        @block.gpsimd
        def _(pool):
            pool.iota(iota_j[:, :], pattern=[[1, SEQ]], base=0, channel_multiplier=0,
                      allow_small_or_imprecise_dtypes=True).then_inc(iota_done, 1)
            pool.memset(mask[:, :], 0.0).then_inc(mask_done, 1)
            pool.wait_ge(mask_done, 1)
            pool.affine_select(out=mask[:, :], in_=mask[:, :], compare_op=ALU.is_ge, fill=NEG, base=0,
                               pattern=[[-1, P]], channel_multiplier=1).then_inc(mask_done, 1)

        @block.vector
        def _(dve):
            dve.wait_ge(consts, 32)
            dve.wait_ge(iota_done, 1)
            with dve.Fori(0, BATCH) as b:
                with dve.Fori(0, TB // 4) as quad:
                    for j in range(4):
                        t = b * TB + quad * 4 + j
                        dve.wait_ge(xT_done, (b * TB + quad * 4) * 1)
                        xt = env.X[:, bass.ds(t, 1), :].rearrange("p a d -> p (a d)")
                        nc.vector.tensor_scalar(xn[:, j, :], xt, env.mean[:, bass.ds(t, 1)],
                                                env.rstd[:, bass.ds(t, 1)], ALU.subtract, ALU.mult).then_inc(xn_done, 1)
                    for j in range(4):
                        t = b * TB + quad * 4 + j
                        xt = env.X[:, bass.ds(t, 1), :].rearrange("p a d -> p (a d)")
                        dve.wait_ge(xn_done, t + 1)
                        nc.vector.tensor_tensor(xt, xt, bo_sb[:, :], ALU.add).then_inc(x_added, 1)
                with dve.Fori(0, PAIRS) as hp:
                    g = b * PAIRS + hp
                    added = b * TB + TB + g * NIB
                    for h in range(2):
                        dve.wait_ge(max_done, g * NCH)
                        nc.vector.tensor_scalar(bias[:, h, :], iota_j[:, :], slope_sb[:, bass.ds(hp * 2 + h, 1)],
                                                -1.0 / SCALE, ALU.mult, ALU.mult).then_inc(bias_done, 1)
                    for v in range(NQK):
                        blk, h, t = v // 4, v // 2 % 2, v % 2
                        cols = slice(blk * BANK, (blk + 1) * BANK)
                        ps = bank((NV + v) % 4)
                        dve.wait_ge(hi_done, g * NQK + v + 1)
                        if t == 0:
                            nc.vector.tensor_tensor(q_st[DH:P, h, cols], ps[DH:P, :], q_st[DH:P, h, cols].bitcast(F32),
                                                    ALU.subtract).then_inc(lo_done, 1)
                        else:
                            nc.vector.tensor_tensor(k_lo[:, h, cols], ps, k_hi[:, h, cols].bitcast(F32),
                                                    ALU.subtract).then_inc(lo_done, 1)
                    dve.wait_ge(bias_done, (g + 1) * 2)
                    for s in range(STEPS):
                        u = s
                        if u < UNITS:
                            h, row = u % 2, u % ROWS
                            if u >= ROWS:
                                dve.wait_ge(probT_done, g * NEV + evac0[u - ROWS + 1])
                            else:
                                dve.wait_ge(probT_done, g * NEV)
                            for i, (a, z) in enumerate(chunks[u]):
                                dve.wait_ge(scores_done, g * NCH + chunk0[u] + i + 1)
                                dve.sem_inc(passed, 1)
                                nc.vector.tensor_tensor_reduce(
                                    out=srow[:, row, a:z], in0=ps_scores(chunk0[u] + i, z - a), in1=bias[:, h, a:z],
                                    scale=1.0, scalar=-3e38, op0=ALU.add, op1=ALU.max,
                                    accum_out=cmax[:, u, i:i + 1]).then_inc(max_done, 1)
                            dve.wait_ge(max_done, g * NCH + chunk0[u + 1])
                            if len(chunks[u]) == 1:
                                nc.vector.tensor_scalar(nmax[:, u:u + 1], cmax[:, u, 0:1], -SCALE, None,
                                                        ALU.mult).then_inc(nmax_done, 1)
                            else:
                                nc.vector.tensor_scalar(nmax[:, u:u + 1], cmax[:, u, 0:1], cmax[:, u, 1:2], -SCALE,
                                                        ALU.max, ALU.mult).then_inc(nmax_done, 1)
                        if 0 <= s - 2 < UNITS:
                            w = s - 2
                            dve.wait_ge(exp_done, g * UNITS + w + 1)
                            nc.vector.reciprocal(zinv[:, w:w + 1], zsum[:, w:w + 1]).then_inc(zinv_done, 1)
                            if w % 2:
                                dve.wait_ge(zinv_done, g * UNITS + w + 1)
                                dve.wait_ge(zT_done, g * NIB + max(w // 4 - 1, 0))
                                nc.vector.tensor_copy(zrep[:, w // 2 % 4, :, :],
                                                      zinv[:, w - 1:w + 1].unsqueeze(2).to_broadcast([P, 2, DH])
                                                      ).then_inc(zrep_done, 1)
                        for ib in range(NIB):
                            if av_step[ib] + 1 == s:
                                dve.wait_ge(av_done, g * NIB + ib + 1)
                                dve.wait_ge(zT_copied, g * NIB + ib + 1)
                                if ib >= 2:
                                    dve.wait_ge(op_done, g * NIB + ib - 1)
                                else:
                                    dve.wait_ge(op_done, g * NIB)
                                nc.vector.tensor_tensor(oT[:, ib % 2, :], bank(6, 0, IB), zT[:, :],
                                                        ALU.mult).then_inc(oT_done, 1)
                            if op_step[ib] + 1 == s:
                                dve.wait_ge(op_done, g * NIB + ib + 1)
                                dve.wait_ge(x_added, added + ib)
                                xt = env.X[:, bass.ds(b * TB + 2 * ib, 2), :].rearrange("p a d -> p (a d)")
                                nc.vector.tensor_tensor(xt, bank(6), xt, ALU.add).then_inc(x_added, 1)
                        if 0 <= s - LAG < UNITS:
                            evacuate(dve, nc.vector.tensor_copy, s - LAG, g, True)
                dve.wait_ge(x_added, (b + 1) * (TB + NIB * PAIRS))

        @block.scalar
        def _(act):
            nc.scalar.preload_act_table_set("exp_and_others")
            with act.Fori(0, BATCH) as b:
                with act.Fori(0, TB // 4) as quad:
                    for c in range(KC):
                        k = (b * (TB // 4) + quad) * KC + c
                        act.wait_ge(xT_done, (b * TB + quad * 4 + 4))
                        nc.scalar.activation(xnT[:, c, bass.ds(quad * BANK, BANK)], bank(4 + c), ACT.Copy
                                             ).then_inc(xT_copied, 1)
                with act.Fori(0, PAIRS) as hp:
                    g = b * PAIRS + hp
                    act.wait_ge(av_done, g * NIB)
                    for v in range(NV):
                        act.wait_ge(proj_done, g * NPROJ + v + 1)
                        nc.scalar.activation(v_sb[:, 4 * v:4 * v + 4, :],
                                             bank(v).rearrange("p (t d) -> p t d", t=4), ACT.Copy).then_inc(v_copied, 1)
                    act.wait_ge(scores_done, g * NCH)
                    for v in range(NQK):
                        blk, h, t = v // 4, v // 2 % 2, v % 2
                        cols = slice(blk * BANK, (blk + 1) * BANK)
                        act.wait_ge(proj_done, g * NPROJ + NV + v + 1)
                        nc.scalar.activation((k_hi if t else q_st)[:, h, cols], bank((NV + v) % 4), ACT.Copy
                                             ).then_inc(hi_done, 1)
                    for s in range(STEPS):
                        if 0 <= s - 1 < UNITS:
                            u = s - 1
                            act.wait_ge(nmax_done, g * UNITS + u + 1)
                            n = (u // 2 + 1) * P
                            nc.scalar.activation(srow[:, u % ROWS, 0:n], srow[:, u % ROWS, 0:n], ACT.Exp,
                                                 bias=nmax[:, u:u + 1], scale=SCALE,
                                                 accum_out=zsum[:, u:u + 1]).then_inc(exp_done, 1)
                        for ib in range(NIB):
                            if av_step[ib] == s:
                                act.wait_ge(av_done, g * NIB + ib + 1)
                                act.wait_ge(oT_done, g * NIB + ib)
                                nc.scalar.activation(zT[:, :], bank(6, IB, BANK), ACT.Copy).then_inc(zT_copied, 1)
                        if 0 <= s - LAG < UNITS:
                            evacuate(act, lambda o, i: nc.scalar.activation(o, i, ACT.Copy), s - LAG, g, False)

        @block.tensor
        def _(pe):
            pe.wait_ge(mask_done, 2)
            with pe.Fori(0, BATCH) as b:
                with pe.Fori(0, TB // 4) as quad:
                    pe.wait_ge(xT_copied, (b * (TB // 4) + quad) * KC)
                    for j in range(4):
                        pe.wait_ge(xn_done, b * TB + quad * 4 + j + 1)
                        for c in range(KC):
                            last = nc.tensor.transpose(bank(4 + c, j * P, (j + 1) * P), xn[:, j, c * P:(c + 1) * P],
                                                       env.ident[:, :])
                        last.then_inc(xT_done, 1)
                pe.wait_ge(xT_copied, (b + 1) * (TB // 4) * KC)
                pe.sem_inc(passed, 1)
                with pe.Fori(0, PAIRS) as hp:
                    g = b * PAIRS + hp
                    pe.wait_ge(w_loaded, (g + 1) * 16 * 5)
                    pe.wait_ge(max_done, g * NCH)
                    for v in range(NV):
                        for t in range(4):
                            for c in range(KC):
                                last = nc.tensor.matmul(bank(v, t * P, (t + 1) * P),
                                                        xnT[:, c, (4 * v + t) * P:(4 * v + t + 1) * P], wv_sb[:, c, :],
                                                        start=(c == 0), stop=(c == KC - 1))
                        last.then_inc(proj_done, 1)
                    for v in range(NQK):
                        blk, h, t = v // 4, v // 2 % 2, v % 2
                        if v < 4:
                            pe.wait_ge(v_copied, g * NV + v + 1)
                        else:
                            pe.wait_ge(lo_done, g * NQK + v - 3)
                        for c in range(KC):
                            last = nc.tensor.matmul(bank((NV + v) % 4),
                                                    wqk_sb[:, h, t, c, :, :].rearrange("p a d -> p (a d)"),
                                                    xnT[:, c, blk * BANK:(blk + 1) * BANK],
                                                    start=(c == 0), stop=(c == KC - 1))
                        last.then_inc(proj_done, 1)
                    pe.wait_ge(lo_done, (g + 1) * NQK)

                    def scores(u):
                        it, h = u // 2, u % 2
                        rows = slice(it * P, (it + 1) * P)
                        for i, (a, z) in enumerate(chunks[u]):
                            c = chunk0[u] + i
                            if c >= 2:
                                pe.wait_ge(max_done, g * NCH + c - 1)
                            for s0 in range(a, z, BANK):
                                s1 = min(s0 + BANK, z)
                                o = ps_scores(c, 2 * BANK)[:, s0 - a:s1 - a]
                                last_one = s1 == (it + 1) * P
                                nc.tensor.matmul(o, q_st[:, h, rows], k_hi[:, h, s0:s1], start=True, stop=False)
                                last = nc.tensor.matmul(o, q_st[:, h, rows], k_lo[:, h, s0:s1], start=False,
                                                        stop=not last_one)
                                if last_one:
                                    last = nc.tensor.matmul(o[:, s1 - s0 - P:s1 - s0], env.ident_bf[:, :], mask[:, :],
                                                            start=False, stop=True)
                            last.then_inc(scores_done, 1)

                    def transposes(u):
                        pe.wait_ge(exp_done, g * UNITS + u + 1)
                        for i, (a, z) in enumerate(evacs[u]):
                            e = evac0[u] + i
                            p = e - 3
                            if p >= 0:
                                if on_dve[p]:
                                    pe.wait_ge(dve_evac, g * n_dve + count(on_dve, p + 1))
                                else:
                                    pe.wait_ge(act_evac, g * n_act + p + 1 - count(on_dve, p + 1))
                            else:
                                pe.wait_ge(dve_evac, g * n_dve)
                                pe.wait_ge(act_evac, g * n_act)
                            for jt in range(a, z):
                                last = nc.tensor.transpose(bank(PT_BANKS[e % 3], (jt - a) * P, (jt - a + 1) * P),
                                                           srow[:, u % ROWS, jt * P:(jt + 1) * P], env.ident[:, :])
                            last.then_inc(probT_done, 1)

                    def product_with_v(ib):
                        e = evac0[4 * (ib + 1)]
                        pe.wait_ge(zrep_done, g * TB + 2 * (ib + 1))
                        pe.wait_ge(x_added, b * TB + TB + g * NIB + ib)
                        for i in range(2):
                            last = nc.tensor.matmul(bank(6, IB + i * P, IB + (i + 1) * P),
                                                    zrep[:, (2 * ib + i) % 4, :, :].rearrange("p h d -> p (h d)"),
                                                    env.ident[:, :], start=(i == 0), stop=True, skip_group_check=True)
                        last.then_inc(zT_done, 1)
                        pe.wait_ge(dve_evac, g * n_dve + count(on_dve, e))
                        pe.wait_ge(act_evac, g * n_act + e - count(on_dve, e))
                        for jt in range(2 * ib + 2):
                            lo = P if jt == 2 * ib + 1 else 0
                            for h in range(2):
                                last = nc.tensor.matmul(bank(6, lo, IB)[h * DH:(h + 1) * DH, :],
                                                        v_sb[:, jt, h * DH:(h + 1) * DH], pT[:, h, jt, lo:IB],
                                                        start=(jt == 0), stop=(jt == 2 * ib + 1), skip_group_check=True)
                        last.then_inc(av_done, 1)

                    def out_projection(ib):
                        if ib == 0:
                            pe.wait_ge(wo_loaded, (g + 1) * 16)
                        pe.wait_ge(oT_done, g * NIB + ib + 1)
                        for i in range(2):
                            last = nc.tensor.matmul(bank(6, i * IB, (i + 1) * IB),
                                                    oT[:, ib % 2, i * P:(i + 1) * P], wo_sb[:, :], start=True, stop=True,
                                                    skip_group_check=True)
                        last.then_inc(op_done, 1)

                    for s in range(STEPS):
                        if s < UNITS:
                            scores(s)
                        for ib in range(NIB):
                            if av_step[ib] == s:
                                product_with_v(ib)
                            if op_step[ib] == s:
                                out_projection(ib)
                        if 0 <= s - LAG < UNITS:
                            transposes(s - LAG)


HB, DB = 16, 16
GUARD = 1e-5
FLOOR = 1e-12
AUG = DB + 2
SPLITS = 7
Q_PARTS, K_PARTS = "hmlhmhl", "hmlmhlh"
KST = SPLITS * AUG
COLS = SEQ
NCHK = TB
HALF = COLS // 2
A_RING, Y_RING = 4, 8
BATCHED = 4
SQUARES = "PAPDPAPDPAPDPAPD"
D_LAG = A_RING - 1
MAX_DIST = 14.4


def stage_attn_b(nc, env, w_qkv, w_o, scalars, ra_scratch, x_scratch):
    with ExitStack() as ctx:
        def sb(n, shape, dt=F32):
            return ctx.enter_context(nc.sbuf_tensor(f"b_{n}", shape, dt))

        def sem(n):
            return env.ctx.enter_context(nc.semaphore(f"b_{n}"))

        tok = sb("tok", [P, 3, TB, D])
        y_ring = sb("y_ring", [P, Y_RING // 2, COLS])
        x_ring = env.X[:, :, :].rearrange("p t d -> p (t d)").rearrange("p (s n) -> p s n", n=COLS)
        a_ring = sb("a_ring", [P, A_RING, COLS])
        xnT = y_ring[:, 0:KC, :]
        xn = y_ring[:, 2, :].rearrange("p (j d) -> p j d", d=D)[:, 0:4, :]
        w_in = y_ring[:, 3, 0:KC * 3 * D].rearrange("p (c n) -> p c n", c=KC)
        sq = a_ring[:, 0, 0:2 * 3 * D].rearrange("p (j n) -> p j n", j=2)
        osq = y_ring[:, 0:2, :].rearrange("p a n -> p (a n)")
        oT = y_ring[:, 2, 0:2 * D].rearrange("p (j n) -> p j n", j=2)
        wo_sb = y_ring[:, 3, 0:KC * D].rearrange("p (c n) -> p c n", c=KC)
        ra_rep = sb("ra_rep", [P, 2, SEQ])
        qT = sb("qT", [KST, 2, SEQ], BF16)
        kT = sb("kT", [KST, 2, SEQ], BF16)
        v_aug = sb("v_aug", [P, 2, TB, 32])
        cap = sb("cap", [P, 2, TB])
        aug = sb("aug", [P, 2, TB, AUG])
        stack = sb("stack", [P, 2, TB, SPLITS, AUG], BF16)
        arr = sb("arr", [P, 4, TB * HB])
        o_sb = sb("o_sb", [P, BANK])
        zinv = sb("zinv", [P, TB])
        sc = sb("sc", [P, 24])
        NS_Q, E_K, EN_K, CAP_K = range(4)
        tmp = a_ring[:, 0, :].rearrange("p (i n) -> p i n", n=TB * HB)
        nsq = a_ring[:, 1, 0:3 * TB * HB].rearrange("p (i n) -> p i n", n=TB * HB)
        ons = a_ring[:, 2, 0:3 * TB * HB].rearrange("p (i n) -> p i n", n=TB * HB)
        raT = a_ring[:, 3, 0:2 * P].rearrange("p (c k) -> p c k", c=2)

        names = ("scal_loaded scal chain w_loaded wo_loaded zeroed xn_done xT_done xT_copied proj_done tok_copied "
                 "sq_done nsq_done root_all x_all th_all ra_done raT_done raT_copied ra_stored ra_loaded0 ra_loaded1 factors_done "
                 "pool_step stack_done grpT_done grp_copied "
                 "x_saved x_back v_ready scores_done scores_read a_ready sq_A sq_D sq_P root_done sum_done ln_done w_done av_done "
                 "o_copied oT_done o_done osq_done osum_done oroot_done o_scaled loT_done loT_copied out_done "
                 "x_added gz_done arr_freed passed").split()
        S = {n: sem(n) for n in names}
        block = ctx.enter_context(nc.Block())

        def bank(i, a=0, b=BANK):
            return env.psum[:, i * BANK + a:i * BANK + b]

        def half_ps(j):
            return env.psum[:, j * 2 * BANK:(j + 1) * 2 * BANK]

        (LOGC, BETA, C, SC, NEG_S, SHIFT, XMAX, ONE, MINUS1, C2, NEG_C) = range(11)

        def col(i, n=1):
            return sc[:, i:i + n]

        def slot(ring, k):
            return k % ring

        def y_slot(k):
            s = k % Y_RING
            return y_ring[:, s, :] if s < Y_RING // 2 else x_ring[:, s - Y_RING // 2, :]

        def av(n):
            return n + Y_RING

        def summed(n):
            return n + A_RING

        def squared(g, k):
            return g * SQUARES.count(SQUARES[k]) + SQUARES[:k].count(SQUARES[k])

        def square_by(eng, engine, name, g, k):
            if SQUARES[k] != name:
                return
            eng.wait_ge(S["a_ready"], g * NCHK + k + 1)
            eng.wait_ge(S["av_done"], g * NCHK + k + 1)
            a = a_ring[:, slot(A_RING, k), :]
            engine.tensor_tensor(y_slot(k), a, a, ALU.mult).then_inc(S["sq_" + name], 1)

        @block.sync
        def _(sp):
            sp.dma_start(sc[:, LOGC:BETA + 1], scalars.to_broadcast([P, 2])).then_inc(S["scal_loaded"], 16)
            with sp.Fori(0, BATCH) as b:
                sp.wait_ge(S["x_added"], b * TB)
                sp.dma_start(w_in, w_qkv.rearrange("(c p) n -> p c n", p=P)).then_inc(S["w_loaded"], 16)
                xs = x_scratch.rearrange("(t p) d -> p t d", p=P)
                for q in range(4):
                    ts = slice(q * NT // 4, (q + 1) * NT // 4)
                    sp.dma_start(xs[:, ts, :], env.X[:, ts, :]).then_inc(S["x_saved"], 16)
                sp.wait_ge(S["raT_copied"], b + 1)
                sp.dma_start(ra_scratch[bass.ds(b, 1)].rearrange("a (c p) k -> p (a c) k", p=P), raT
                             ).then_inc(S["ra_stored"], 16)
                sp.wait_ge(S["ra_stored"], (b + 1) * 16)

                def load_ra(h, j):
                    g = b * HB + h
                    if not (isinstance(h, int) and h < 2):
                        sp.wait_ge(S["scores_read"], (g - 1) * 2 * NCHK)
                    else:
                        sp.wait_ge(S["scores_read"], b * HB * 2 * NCHK)
                    src = ra_scratch[bass.ds(b, 1)].rearrange("a (t h) k -> (a h) t k", h=HB)[bass.ds(h, 1)]
                    sp.dma_start(ra_rep[:, j, :].rearrange("p (t k) -> p t k", k=P), src.to_broadcast([P, TB, P])
                                 ).then_inc(S[f"ra_loaded{j}"], 16)

                load_ra(0, 0)
                load_ra(1, 1)
                with sp.Fori(0, HB // 2 - 1) as i:
                    load_ra(i * 2 + 2, 0)
                    load_ra(i * 2 + 3, 1)
                sp.wait_ge(S["av_done"], av((b + 1) * HB * NCHK))
                sp.dma_start(wo_sb, w_o.rearrange("(c p) n -> p c n", p=P)).then_inc(S["wo_loaded"], 16)
                sp.wait_ge(S["x_saved"], (b + 1) * 64)
                for q in range(4):
                    ts = slice(q * NT // 4, (q + 1) * NT // 4)
                    sp.dma_start(env.X[:, ts, :], xs[:, ts, :]).then_inc(S["x_back"], 16)
                sp.wait_ge(S["x_back"], (b + 1) * 64)
                sp.sem_inc(S["passed"], 1)

        @block.gpsimd
        def _(pool):
            count = [0]
            nc.gpsimd.memset(v_aug[:, :, :, :], 0.0).then_inc(S["zeroed"], 1)
            pool.wait_ge(S["zeroed"], 1)
            nc.gpsimd.memset(v_aug[:, :, :, DB:DB + 1], 1.0).then_inc(S["zeroed"], 1)
            pool.wait_ge(S["zeroed"], 2)
            PREP = 20

            def prep(b, h, j, squares=False):
                g = b * HB + h
                todo = [k for k in range(NCHK) if SQUARES[k] == "P"] if squares else []
                early = [k for k in todo if k < NCHK // 2 - 1]
                every = PREP // (len(early) + 1)
                n = [0]

                def step(ins):
                    n[0] += 1
                    ins.then_inc(S["pool_step"], 1)
                    if todo and todo[0] in early and n[0] % every == 0:
                        square_by(pool, nc.gpsimd, "P", g - 1, todo.pop(0))

                def sync():
                    pool.wait_ge(S["pool_step"], g * PREP + n[0])
                    pool.sem_inc(S["passed"], 1)

                def of(i):
                    return arr[:, i, :].rearrange("p (t h) -> p t h", h=HB)[:, :, bass.ds(h, 1)]

                def toks(i):
                    return tok[:, i, :, :].rearrange("p t (h d) -> p t h d", d=DB)[:, :, bass.ds(h, 1), :].rearrange(
                        "p t a d -> p t (a d)")

                if not (isinstance(h, int) and h < 2):
                    pool.wait_ge(S["scores_read"], (g - 1) * 2 * NCHK)
                    pool.sem_inc(S["passed"], 1)
                step(nc.gpsimd.tensor_copy(cap[:, j, :].unsqueeze(2), of(CAP_K)))
                step(nc.gpsimd.tensor_copy(aug[:, 0, :, 0:DB], toks(0)))
                step(nc.gpsimd.tensor_copy(aug[:, 0, :, DB:DB + 1], of(NS_Q)))
                step(nc.gpsimd.memset(aug[:, 0, :, DB + 1:AUG], 1.0))
                step(nc.gpsimd.tensor_copy(aug[:, 1, :, 0:DB], toks(1)))
                step(nc.gpsimd.tensor_copy(aug[:, 1, :, DB:DB + 1], of(E_K)))
                step(nc.gpsimd.tensor_copy(aug[:, 1, :, DB + 1:AUG], of(EN_K)))
                sync()
                pool.wait_ge(S["grpT_done"], g * 4)
                pool.sem_inc(S["passed"], 1)
                a2 = aug[:, :, :, :].rearrange("p a t d -> p (a t) d")
                s2 = stack[:, :, :, :, :].rearrange("p a t s d -> p (a t) s d")
                for i in range(3):
                    step(nc.gpsimd.tensor_copy(s2[:, :, i, :], a2))
                    sync()
                    if i < 2:
                        step(nc.gpsimd.tensor_tensor(a2, a2, s2[:, :, i, :], ALU.subtract))
                        sync()
                for i, order in enumerate((Q_PARTS, K_PARTS)):
                    for n_s in range(3, SPLITS):
                        step(nc.gpsimd.tensor_copy(stack[:, i, :, n_s, :], stack[:, i, :, "hml".index(order[n_s]), :]))
                sync()
                assert n[0] == PREP, n[0]
                pool.sem_inc(S["stack_done"], 1)
                while todo:
                    square_by(pool, nc.gpsimd, "P", g - 1, todo.pop(0))
                if not (isinstance(h, int) and h < 2):
                    pool.wait_ge(S["av_done"], av((g - 1) * NCHK))
                    pool.sem_inc(S["passed"], 1)
                nc.gpsimd.tensor_copy(v_aug[:, j, :, 0:DB], toks(2)).then_inc(S["v_ready"], 1)

            with pool.Fori(0, BATCH) as b:
                pool.wait_ge(S["factors_done"], b + 1)
                pool.sem_inc(S["passed"], 1)
                prep(b, 0, 0)
                pool.wait_ge(S["x_saved"], (b + 1) * 64)
                pool.sem_inc(S["passed"], 1)
                prep(b, 1, 1, squares=True)
                with pool.Fori(0, HB // 2 - 1) as i:
                    prep(b, i * 2 + 2, 0, squares=True)
                    prep(b, i * 2 + 3, 1, squares=True)
                for k in range(NCHK):
                    square_by(pool, nc.gpsimd, "P", b * HB + HB - 1, k)

        @block.vector
        def _(dve):
            n_chain = [0]

            def link(ins):
                n_chain[0] += 1
                ins.then_inc(S["chain"], 1)
                dve.wait_ge(S["chain"], n_chain[0])

            T = 11
            dve.sem_inc(S["sum_done"], A_RING)
            dve.wait_ge(S["scal_loaded"], 16)
            link(nc.vector.memset(col(ONE), 1.0))
            link(nc.vector.memset(col(MINUS1), -1.0))
            link(nc.vector.tensor_scalar(col(T, 2), col(LOGC, 2), -1.0, None, ALU.mult))
            link(nc.vector.tensor_tensor(col(T, 2), col(T, 2), col(LOGC, 2), ALU.min))
            nc.vector.tensor_copy(col(T, 2), col(T, 2)).then_inc(S["gz_done"], 1)
            dve.wait_ge(S["scal"], 2)
            link(nc.vector.tensor_scalar(col(T, 2), col(T + 2, 2), 1.0, -1.0, ALU.add, ALU.add))
            link(nc.vector.tensor_scalar(col(T + 6, 2), col(T, 2), 0.0, None, ALU.is_equal))
            link(nc.vector.tensor_tensor(col(T, 2), col(T, 2), col(T + 6, 2), ALU.add))
            link(nc.vector.reciprocal(col(T, 2), col(T, 2)))
            link(nc.vector.tensor_tensor(col(T, 2), col(T, 2), col(T + 4, 2), ALU.mult))
            link(nc.vector.tensor_tensor(col(T, 2), col(T, 2), col(T + 6, 2), ALU.add))
            link(nc.vector.tensor_tensor(col(T, 2), col(T, 2), col(T + 2, 2), ALU.mult))
            link(nc.vector.tensor_scalar(col(T + 4, 2), col(LOGC, 2), 0.0, None, ALU.max))
            link(nc.vector.tensor_tensor(col(T, 2), col(T, 2), col(T + 4, 2), ALU.add))
            link(nc.vector.tensor_copy(col(C), col(T)))
            link(nc.vector.tensor_scalar(col(C2), col(T), 2.0, None, ALU.mult))
            link(nc.vector.tensor_scalar(col(NEG_C), col(T), -1.0, None, ALU.mult))
            nc.vector.tensor_copy(col(T + 8), col(T)).then_inc(S["gz_done"], 1)
            dve.wait_ge(S["scal"], 3)
            link(nc.vector.reciprocal(col(T + 2), col(SC)))
            link(nc.vector.tensor_tensor(col(T + 3), col(T + 1), col(T + 2), ALU.mult))
            link(nc.vector.tensor_scalar(col(NEG_S), col(T + 3), -1.0, None, ALU.mult))
            link(nc.vector.tensor_scalar(col(SHIFT), col(T + 3), MAX_DIST / 2, None, ALU.mult))
            link(nc.vector.tensor_scalar(col(T + 4), col(SC), GUARD, None, ALU.mult))
            link(nc.vector.reciprocal(col(T + 5), col(T + 4)))
            link(nc.vector.tensor_scalar(col(T + 6), col(T + 4), -1.0, 2.0, ALU.mult, ALU.add))
            link(nc.vector.tensor_tensor(col(T + 6), col(T + 6), col(T + 5), ALU.mult))
            nc.vector.tensor_copy(col(T + 7), col(T + 6)).then_inc(S["gz_done"], 1)
            dve.wait_ge(S["scal"], 4)
            link(nc.vector.tensor_scalar(col(XMAX), col(T + 9), 0.5, None, ALU.mult))
            n0 = n_chain[0]
            FACTORS = 24
            base = [None, 0]

            def chained(ins):
                base[1] += 1
                ins.then_inc(S["chain"], 1)
                dve.wait_ge(S["chain"], base[0] + base[1])

            def t3(x):
                return x.rearrange("p t (h d) -> p t h d", d=DB)

            with dve.Fori(0, BATCH) as b:
                base[0], base[1] = b * FACTORS + n0, 0
                dve.wait_ge(S["x_added"], b * TB)
                for t in range(TB):
                    if t >= 4:
                        dve.wait_ge(S["xT_done"], b * TB + t - 3)
                    nc.vector.tensor_scalar(xn[:, t % 4, :], env.X[:, bass.ds(b * TB + t, 1), :].rearrange("p a d -> p (a d)"),
                                            env.mean[:, bass.ds(b * TB + t, 1)], env.rstd[:, bass.ds(b * TB + t, 1)],
                                            ALU.subtract, ALU.mult).then_inc(S["xn_done"], 1)
                nh = nsq.rearrange("p a (t h) -> p a t h", h=HB)
                for t in range(TB):
                    dve.wait_ge(S["sq_done"], b * TB + t + 1)
                    nc.vector.reduce_sum(nh[:, :, t, :], sq[:, t % 2, :].rearrange("p (a h d) -> p a h d", a=3, d=DB),
                                         AX.X).then_inc(S["nsq_done"], 1)
                dve.wait_ge(S["root_all"], b + 1)
                x2, f2, n2 = tmp[:, 0:2, :], tmp[:, 3:5, :], tmp[:, 5:7, :]
                chained(nc.vector.tensor_scalar(x2, x2, GUARD, col(SC), ALU.max, ALU.mult))
                nc.vector.tensor_scalar(tmp[:, 2, :], tmp[:, 2, :], col(SC), 1e-30, ALU.mult, ALU.max).then_inc(S["x_all"], 1)
                dve.wait_ge(S["th_all"], b + 1)
                chained(nc.vector.reciprocal(x2, x2))
                chained(nc.vector.tensor_tensor(f2, f2, x2, ALU.mult))
                chained(nc.vector.tensor_tensor(n2, f2, f2, ALU.mult))
                chained(nc.vector.tensor_tensor(n2, n2, nsq[:, 0:2, :], ALU.mult))
                nc.vector.tensor_copy(arr[:, NS_Q, :], n2[:, 0, :])
                chained(nc.vector.tensor_scalar(x2, n2, col(NEG_C), 1.0, ALU.mult, ALU.add))
                chained(nc.vector.tensor_scalar(x2, x2, FLOOR, None, ALU.max))
                nc.vector.tensor_scalar(arr[:, CAP_K, :], x2[:, 1, :], 1.0 / GUARD, None, ALU.mult)
                chained(nc.vector.reciprocal(tmp[:, 7, :], x2[:, 1, :]))
                nc.vector.reciprocal(ons[:, 2, :], x2[:, 0, :]).then_inc(S["ra_done"], 1)
                chained(nc.vector.tensor_scalar(arr[:, E_K, :], tmp[:, 7, :], col(C2), None, ALU.mult))
                nc.vector.tensor_tensor(arr[:, EN_K, :], n2[:, 1, :], arr[:, E_K, :], ALU.mult)
                chained(nc.vector.tensor_tensor(f2[:, 1, :], f2[:, 1, :], arr[:, E_K, :], ALU.mult))
                chained(nc.vector.tensor_scalar(f2[:, 1, :], f2[:, 1, :], -2.0, None, ALU.mult))
                chained(nc.vector.reciprocal(tmp[:, 2, :], tmp[:, 2, :]))
                chained(nc.vector.tensor_scalar(tmp[:, 2, :], tmp[:, 2, :], col(XMAX), 1.0, ALU.mult, ALU.min))
                for i, f in enumerate((3, 4, 2)):
                    dst = tok[:, i, :, :].rearrange("p t n -> p (t n)").rearrange("p (n d) -> p n d", d=DB)
                    chained(nc.vector.tensor_tensor(dst, dst, tmp[:, f, :].unsqueeze(2).to_broadcast([P, TB * HB, DB]),
                                                    ALU.mult))
                dve.sem_inc(S["factors_done"], 1)

                def root_sum(g, k):
                    n = g * NCHK + k
                    dve.wait_ge(S["root_done"], n + 1)
                    kk = k % NCHK
                    y = y_slot(kk)
                    nc.vector.tensor_tensor(y, a_ring[:, slot(A_RING, kk), :], y, ALU.add).then_inc(S["sum_done"], 1)

                def argument(g, k, j):
                    a = a_ring[:, slot(A_RING, k), :]
                    dve.wait_ge(S["sum_done"], g * NCHK + k + 1)
                    for s in range(2):
                        dve.wait_ge(S["scores_done"], g * 2 * NCHK + 2 * k + s + 1)
                        nc.vector.scalar_tensor_tensor(out=a[:, s * HALF:(s + 1) * HALF],
                                                       in0=ra_rep[:, j, s * HALF:(s + 1) * HALF], scalar=cap[:, j, k:k + 1],
                                                       in1=half_ps(s), op0=ALU.min, op1=ALU.mult).then_inc(S["scores_read"], 1)

                def clamp(g, k):
                    a = a_ring[:, slot(A_RING, k), :]
                    dve.wait_ge(S["scores_read"], g * 2 * NCHK + 2 * k + 2)
                    nc.vector.tensor_scalar(a, a, 1.0, 1.0 + GUARD, ALU.add, ALU.max).then_inc(S["a_ready"], 1)

                def group_copied(g, i, j):
                    dve.wait_ge(S["grpT_done"], g * 4 + i + 1)
                    dst = (qT, kT)[i // 2][:, j, (i % 2) * 1024:(i % 2 + 1) * 1024]
                    nc.vector.tensor_copy(dst, bank(6 + (i + 1) % 2).bitcast(BF16)[0:KST, :]).then_inc(S["grp_copied"], 1)

                def out_copy(g):
                    dve.wait_ge(S["av_done"], av((g + 1) * NCHK))
                    dve.wait_ge(S["oT_done"], g)
                    nc.vector.tensor_copy(o_sb[:, :], out_bank(g_par)).then_inc(S["o_copied"], 1)

                def out_scale(g, h):
                    dve.wait_ge(S["oT_done"], g + 1)
                    o = bank(6).rearrange("p (c i d) -> p i c d", c=4, i=4)
                    z = zinv[:, :].rearrange("p (i c) -> p i c", c=4)
                    nc.vector.reciprocal(z.unsqueeze(3), o[:, :, :, DB:DB + 1]).then_inc(S["arr_freed"], 1)
                    dve.wait_ge(S["arr_freed"], g + 1)
                    for i in range(4):
                        dst = t3(tok[:, 0, 4 * i:4 * i + 4, :])[:, :, bass.ds(h, 1), :].rearrange("p t a d -> p t (a d)")
                        last = nc.vector.tensor_tensor(dst, o[:, i, :, 0:DB],
                                                       z[:, i, :].unsqueeze(2).to_broadcast([P, 4, DB]), ALU.mult)
                        last.then_inc(S["o_done"], 1)

                def out_bank(par):
                    return bank(4 + par)

                for i in range(4):
                    group_copied(b * HB, i, 0)
                dve.wait_ge(S["grp_copied"], b * HB * 4 + 4)

                def head(h, j, first, last):
                    nonlocal g_par
                    g = b * HB + h
                    dve.wait_ge(S[f"ra_loaded{j}"], (g - j) * 8 + 16)
                    dve.wait_ge(S["pool_step"], g * 20 + 20)
                    for k in range(NCHK):
                        argument(g, k, j)
                        if k % BATCHED == BATCHED - 1:
                            clamp(g, k)
                            for m in range(k + 1 - BATCHED, k + 1):
                                square_by(dve, nc.vector, "D", g, m)
                            root_sum(g, k - D_LAG)
                        else:
                            if k >= D_LAG or not first:
                                root_sum(g, k - D_LAG)
                            clamp(g, k)
                        if not first and k == 9:
                            g_par = 1 - j
                            out_copy(g - 1)
                        if not first and k == 11:
                            out_scale(g - 1, h - 1)
                        if not last and 11 <= k < 15:
                            group_copied(g + 1, k - 11, 1 - j)

                g_par = 0
                dve.wait_ge(S["x_saved"], (b + 1) * 64)
                head(0, 0, True, False)
                with dve.Fori(0, HB // 2 - 1) as i:
                    head(i * 2 + 1, 1, False, False)
                    head(i * 2 + 2, 0, False, False)
                head(HB - 1, 1, False, True)
                g = b * HB + HB
                for k in range(NCHK - D_LAG, NCHK):
                    root_sum(g, k - NCHK)
                g_par = 1
                out_copy(g - 1)
                out_scale(g - 1, HB - 1)
                dve.wait_ge(S["o_done"], g * 4)
                o_all = tok[:, 0, :, :].rearrange("p t n -> p (t n)")
                dve.wait_ge(S["av_done"], av(g * NCHK))
                nc.vector.tensor_tensor(osq, o_all, o_all, ALU.mult).then_inc(S["osq_done"], 1)
                dve.wait_ge(S["osq_done"], b + 1)
                nc.vector.reduce_sum(ons[:, 0, :], osq.rearrange("p (n d) -> p n d", d=DB), AX.X).then_inc(S["osum_done"], 1)
                dve.wait_ge(S["oroot_done"], b + 1)
                chained(nc.vector.tensor_scalar(ons[:, 1, :], ons[:, 1, :], col(SC), 1e-30, ALU.mult, ALU.max))
                chained(nc.vector.reciprocal(ons[:, 0, :], ons[:, 1, :]))
                chained(nc.vector.tensor_scalar(ons[:, 1, :], ons[:, 0, :], col(XMAX), 1.0, ALU.mult, ALU.min))
                o3 = o_all.rearrange("p (n d) -> p n d", d=DB)
                nc.vector.tensor_tensor(o3, o3, ons[:, 1, :].unsqueeze(2).to_broadcast([P, TB * HB, DB]), ALU.mult
                                        ).then_inc(S["o_scaled"], 1)
                for t in range(TB):
                    dve.wait_ge(S["out_done"], b * TB + t + 1)
                    dve.wait_ge(S["x_back"], (b + 1) * 64)
                    xt = env.X[:, bass.ds(b * TB + t, 1), :].rearrange("p a d -> p (a d)")
                    nc.vector.tensor_tensor(xt, bank(2 + t % 2, 0, D), xt, ALU.add).then_inc(S["x_added"], 1)
                while base[1] < FACTORS:
                    chained(nc.vector.tensor_copy(col(T + 10), col(ONE)))
                assert base[1] == FACTORS, base[1]
                dve.wait_ge(S["x_added"], (b + 1) * TB)

        @block.scalar
        def _(act):
            act.wait_ge(S["gz_done"], 1)
            T = 11
            nc.scalar.activation(col(T + 2, 2), col(T, 2), ACT.Exp).then_inc(S["scal"], 1)
            act.wait_ge(S["scal"], 1)
            nc.scalar.activation(col(T + 4, 2), col(T + 2, 2), ACT.Ln, bias=col(ONE)).then_inc(S["scal"], 1)
            act.wait_ge(S["gz_done"], 2)
            nc.scalar.activation(col(SC), col(C), ACT.Sqrt).then_inc(S["scal"], 1)
            act.wait_ge(S["gz_done"], 3)
            nc.scalar.activation(col(T + 9), col(T + 7), ACT.Ln).then_inc(S["scal"], 1)
            with act.Fori(0, BATCH) as b:
                act.wait_ge(S["x_added"], b * TB)
                for q in range(TB // 4):
                    act.wait_ge(S["xT_done"], b * TB + 4 * q + 4)
                    for c in range(KC):
                        nc.scalar.activation(xnT[:, c, q * BANK:(q + 1) * BANK], bank(4 + c), ACT.Copy
                                             ).then_inc(S["xT_copied"], 1)
                for t in range(TB):
                    act.wait_ge(S["proj_done"], b * TB + t + 1)
                    ps = half_ps(t % 2)[:, 0:3 * D]
                    if t >= 2:
                        act.wait_ge(S["nsq_done"], b * TB + t - 1)
                    nc.scalar.activation(sq[:, t % 2, :], ps, ACT.Square).then_inc(S["sq_done"], 1)
                    nc.scalar.activation(tok[:, :, t, :], ps.rearrange("p (a n) -> p a n", a=3), ACT.Copy
                                         ).then_inc(S["tok_copied"], 1)
                act.wait_ge(S["nsq_done"], (b + 1) * TB)
                nc.scalar.activation(tmp[:, 0:3, :], nsq, ACT.Sqrt).then_inc(S["root_all"], 1)
                act.wait_ge(S["x_all"], b + 1)
                nc.scalar.activation(tmp[:, 3:5, :], tmp[:, 0:2, :], ACT.Tanh).then_inc(S["th_all"], 1)
                act.wait_ge(S["raT_done"], b + 1)
                nc.scalar.activation(raT, bank(6, 0, 2 * P).rearrange("p (c k) -> p c k", c=2), ACT.Copy
                                     ).then_inc(S["raT_copied"], 1)

                def square(g, k):
                    if SQUARES[k] != "A":
                        return
                    act.wait_ge(S["a_ready"], g * NCHK + k + 1)
                    act.wait_ge(S["av_done"], g * NCHK + k + 1)
                    nc.scalar.activation(y_slot(k), a_ring[:, slot(A_RING, k), :], ACT.Square).then_inc(S["sq_A"], 1)

                def root(g, k):
                    act.wait_ge(S["sq_" + SQUARES[k]], squared(g, k) + 1)
                    nc.scalar.activation(y_slot(k), y_slot(k), ACT.Sqrt, bias=col(MINUS1)).then_inc(S["root_done"], 1)

                def log(g, k):
                    act.wait_ge(S["sum_done"], summed(g * NCHK + k + 1))
                    nc.scalar.activation(y_slot(k), y_slot(k), ACT.Ln).then_inc(S["ln_done"], 1)

                def weight(g, k):
                    act.wait_ge(S["ln_done"], g * NCHK + k + 1)
                    nc.scalar.activation(y_slot(k), y_slot(k), ACT.Exp, bias=col(SHIFT), scale=col(NEG_S)
                                         ).then_inc(S["w_done"], 1)

                def batch(first, second, g, n):
                    ks = range(n * BATCHED, (n + 1) * BATCHED)
                    for k in ks:
                        first(g, k)
                        if k > ks[0]:
                            second(g, k - 1)
                    second(g, ks[-1])

                def roots(g, n):
                    batch(square, root, g, n)

                def weights(g, n):
                    nc.scalar.preload_act_table_set("natural_log_exp_and_others")
                    batch(log, weight, g, n)

                NB = NCHK // BATCHED
                act.wait_ge(S["x_saved"], (b + 1) * 64)
                roots(b * HB, 0)
                with act.Fori(0, HB - 1) as h:
                    for n in range(NB):
                        roots(b * HB + h + (n + 1) // NB, (n + 1) % NB)
                        weights(b * HB + h, n)
                for n in range(NB):
                    if n + 1 < NB:
                        roots(b * HB + HB - 1, n + 1)
                    weights(b * HB + HB - 1, n)
                g = b * HB + HB
                act.wait_ge(S["osum_done"], b + 1)
                nc.scalar.activation(ons[:, 1, :], ons[:, 0, :], ACT.Sqrt).then_inc(S["oroot_done"], 1)
                for t in range(TB):
                    act.wait_ge(S["loT_done"], b * TB + t + 1)
                    if t >= 2:
                        act.wait_ge(S["out_done"], b * TB + t - 1)
                    nc.scalar.activation(oT[:, t % 2, :], bank(t % 2, 0, D), ACT.Copy).then_inc(S["loT_copied"], 1)

        @block.tensor
        def _(pe):
            pe.sem_inc(S["av_done"], Y_RING)
            with pe.Fori(0, BATCH) as b:
                for t in range(TB):
                    if t % 4 == 0:
                        pe.wait_ge(S["xT_copied"], (b * (TB // 4) + t // 4) * KC)
                    pe.wait_ge(S["xn_done"], b * TB + t + 1)
                    for c in range(KC):
                        last = nc.tensor.transpose(bank(4 + c, t % 4 * P, (t % 4 + 1) * P), xn[:, t % 4, c * P:(c + 1) * P],
                                                   env.ident[:, :])
                    last.then_inc(S["xT_done"], 1)
                pe.wait_ge(S["xT_copied"], (b + 1) * (TB // 4) * KC)
                pe.wait_ge(S["w_loaded"], (b + 1) * 16)
                for t in range(TB):
                    if t >= 2:
                        pe.wait_ge(S["tok_copied"], b * TB + t - 1)
                    for a, z in ((0, BANK), (BANK, 3 * D)):
                        for c in range(KC):
                            last = nc.tensor.matmul(half_ps(t % 2)[:, a:z], xnT[:, c, t * P:(t + 1) * P], w_in[:, c, a:z],
                                                    start=(c == 0), stop=(c == KC - 1))
                    last.then_inc(S["proj_done"], 1)
                pe.wait_ge(S["ra_done"], b + 1)
                for c in range(2):
                    last = nc.tensor.transpose(bank(6, c * P, (c + 1) * P), ons[:, 2, c * P:(c + 1) * P], env.ident[:, :])
                last.then_inc(S["raT_done"], 1)
                pe.wait_ge(S["tok_copied"], (b + 1) * TB)
                pe.wait_ge(S["raT_copied"], b + 1)

                def group(g, i, j):
                    if i == 0:
                        pe.wait_ge(S["stack_done"], g + 1)
                    pe.wait_ge(S["grp_copied"], g * 4 + max(i - 1, 0))
                    ps = bank(6 + (i + 1) % 2).bitcast(BF16)
                    for t in range(8):
                        src = stack[:, i // 2, (i % 2) * 8 + t, :, :].rearrange("p s d -> p (s d)")
                        last = nc.tensor.transpose(ps[0:KST, t * P:(t + 1) * P], src, env.ident_bf[:, :])
                    last.then_inc(S["grpT_done"], 1)

                def scores(g, k, j, first):
                    for s in range(2):
                        n = g * 2 * NCHK + 2 * k + s
                        if first and k == 0:
                            pe.wait_ge(S["scores_read"], g * 2 * NCHK)
                        elif k > 0:
                            pe.wait_ge(S["scores_read"], n - 1)
                        else:
                            pe.wait_ge(S["scores_read"], g * 2 * NCHK - (1 - s))
                        for i in range(2):
                            cs = slice(s * HALF + i * BANK, s * HALF + (i + 1) * BANK)
                            last = nc.tensor.matmul(half_ps(s)[:, i * BANK:(i + 1) * BANK], kT[:, j, k * P:(k + 1) * P],
                                                    qT[:, j, cs], start=True, stop=True)
                        last.then_inc(S["scores_done"], 1)

                def product(g, k, j):
                    pe.wait_ge(S["w_done"], g * NCHK + k + 1)
                    if k == 0:
                        pe.wait_ge(S["v_ready"], g + 1)
                        pe.wait_ge(S["o_copied"], g_before(g))
                    for i in range(4):
                        last = nc.tensor.matmul(bank(4 + j)[32 * i:32 * i + 32, :], v_aug[:, j, k, :],
                                                y_slot(k)[:, i * BANK:(i + 1) * BANK],
                                                start=(k == 0), stop=(k == NCHK - 1), skip_group_check=True)
                    last.then_inc(S["av_done"], 1)

                def products_after(k):
                    return {BATCHED - 2: [k - 10], BATCHED - 1: [k - 10, k - 9, k - 8]}.get(k % BATCHED, [])

                def g_before(g):
                    return g_first[0] if g_first[0] is not None else g - 1

                g_first = [None]

                def out_transposes(g):
                    pe.wait_ge(S["o_copied"], g + 1)
                    for c in range(4):
                        last = nc.tensor.transpose(bank(6, c * P, (c + 1) * P), o_sb[:, c * P:(c + 1) * P], env.ident[:, :])
                    last.then_inc(S["oT_done"], 1)

                for i in range(4):
                    group(b * HB, i, 0)
                pe.wait_ge(S["grp_copied"], b * HB * 4 + 4)

                def head(h, j, first, last):
                    g = b * HB + h
                    for k in range(NCHK):
                        scores(g, k, j, first)
                        for m in products_after(k):
                            if m >= 0:
                                g_first[0] = b * HB if first else None
                                product(g, m, j)
                                g_first[0] = None
                            elif not first:
                                product(g - 1, m + NCHK, 1 - j)
                        if not first and k == 10:
                            out_transposes(g - 1)
                        if not last and 11 <= k < 15:
                            if k == 12:
                                pe.wait_ge(S["o_done"], g * 4)
                                pe.wait_ge(S["scores_read"], g * 2 * NCHK)
                            group(g + 1, k - 11, 1 - j)
                    if not last:
                        pe.wait_ge(S["grp_copied"], (g + 2) * 4)
                        pe.sem_inc(S["passed"], 1)

                head(0, 0, True, False)
                with pe.Fori(0, HB // 2 - 1) as i:
                    head(i * 2 + 1, 1, False, False)
                    head(i * 2 + 2, 0, False, False)
                head(HB - 1, 1, False, True)
                g = b * HB + HB
                for k in range(NCHK - Y_RING, NCHK):
                    product(g - 1, k, 1)
                out_transposes(g - 1)
                pe.wait_ge(S["o_scaled"], b + 1)
                pe.wait_ge(S["wo_loaded"], (b + 1) * 16)
                for t in range(TB):
                    if t >= 2:
                        pe.wait_ge(S["loT_copied"], b * TB + t - 1)
                    for c in range(KC):
                        last = nc.tensor.transpose(bank(t % 2, c * P, (c + 1) * P), tok[:, 0, t, c * P:(c + 1) * P],
                                                   env.ident[:, :])
                    last.then_inc(S["loT_done"], 1)
                    pe.wait_ge(S["loT_copied"], b * TB + t + 1)
                    if t >= 2:
                        pe.wait_ge(S["x_added"], b * TB + t - 1)
                    for c in range(KC):
                        last = nc.tensor.matmul(bank(2 + t % 2, 0, D), oT[:, t % 2, c * P:(c + 1) * P], wo_sb[:, c, :],
                                                start=(c == 0), stop=(c == KC - 1))
                    last.then_inc(S["out_done"], 1)
                pe.wait_ge(S["x_added"], (b + 1) * TB)


def program(nc, x, wqk, wv, wo, bo, slopes, w_cat, right_aug, w_qkv, w_o, scalars, out):
    ra_scratch = nc.dram_tensor("ra_scratch", (BATCH, TB * HB, P), F32).ap()
    x_scratch = nc.dram_tensor("x_scratch", (BATCH * SEQ, D), F32).ap()
    with ExitStack() as ctx:
        env = make_env(nc, ctx)
        stage_load(nc, env, x)
        stage_ln_stats(nc, env, "ln0")
        stage_attn_a(nc, env, wqk, wv, wo, bo, slopes)
        stage_ln_stats(nc, env, "ln1")
        stage_ffn(nc, env, "ffn0", w_cat, right_aug)
        stage_ln_stats(nc, env, "ln2")
        stage_attn_b(nc, env, w_qkv, w_o, scalars, ra_scratch, x_scratch)
        stage_ln_stats(nc, env, "ln3")
        stage_ffn(nc, env, "ffn1", w_cat, right_aug, out=out)


def kernel(**inputs):
    import numpy as np
    import concourse.bacc as _bacc
    from concourse.bass_utils import run_bass_kernel_spmd as _run

    i = {k[3:]: np.asarray(v) for k, v in inputs.items()}
    wqk = np.stack([i[n].reshape(KC, P, HA, DH).transpose(2, 1, 0, 3) for n in ("attn_a_Wq", "attn_a_Wk")], 2)
    base = np.float32((2.0 ** 8) ** (1.0 / HA))
    slopes = (np.float32(1.0) / base ** np.arange(1, HA + 1, dtype=np.float32)).reshape(1, HA)
    arrays = {
        "x": i["attn_a_x"].reshape(BATCH * SEQ, D),
        "wqk": wqk,
        "wv": i["attn_a_Wv"].reshape(KC, P, PAIRS, 2 * DH).transpose(2, 1, 0, 3),
        "wo": i["attn_a_Wo"].reshape(PAIRS, 2 * DH, D),
        "bo": i["attn_a_bo"].reshape(1, D),
        "slopes": slopes,
        "w_cat": np.concatenate([i["ffn_W_lin"].T, i["ffn_gate_w"].T, i["ffn_left"].transpose(1, 0, 2).reshape(D, E * R)], 1),
        "right_aug": np.concatenate([i["ffn_right"].reshape(E * R, D), i["ffn_b_lin"].reshape(1, D)], 0),
        "w_qkv": np.concatenate([i["attn_b_W_q"].T, i["attn_b_W_k"].T, i["attn_b_W_v"].T], 1),
        "w_o": i["attn_b_W_o"].T,
        "scalars": np.stack([i["attn_b_log_c"], i["attn_b_beta"]]).reshape(1, 2),
    }
    nc = _bacc.Bacc("TRN2", target_bir_lowering=False, num_devices=1)
    fed, args = {}, {}
    for name, a in arrays.items():
        a = np.ascontiguousarray(a)
        fed[f"in_{name}_dram"] = a
        args[name] = nc.dram_tensor(f"in_{name}_dram", a.shape, F32, kind="ExternalInput").ap()
    args["out"] = nc.dram_tensor("out_0_dram", (BATCH * SEQ, D), F32, kind="ExternalOutput").ap()
    program(nc, **args)
    r = _run(nc, [fed], core_ids=[0])
    return r.results[0]["out_0_dram"].reshape(BATCH, SEQ, D)
```

```python
from contextlib import ExitStack

import concourse.bass as bass
from concourse import mybir

F32 = mybir.dt.float32
F32R = mybir.dt.float32r
BF16 = mybir.dt.bfloat16
U32 = mybir.dt.uint32
ALU = mybir.AluOpType
ACT = mybir.ActivationFunctionType
AX = mybir.AxisListType

P = 128
BATCH, SEQ, D = 2, 2048, 256
TB = SEQ // P
NT = BATCH * TB
KC = D // P
LN_EPS = 1e-5
BANK = 512


class Env:
    pass


def make_env(nc, ctx):
    e = Env()
    e.ctx = ctx
    e.X = ctx.enter_context(nc.sbuf_tensor("X", [P, NT, D], F32))
    e.ident = ctx.enter_context(nc.sbuf_tensor("ident", [P, P], F32))
    e.ident_bf = ctx.enter_context(nc.sbuf_tensor("ident_bf", [P, P], BF16))
    e.mean = ctx.enter_context(nc.sbuf_tensor("ln_mean", [P, NT], F32))
    e.rstd = ctx.enter_context(nc.sbuf_tensor("ln_rstd", [P, NT], F32))
    e.ln_eps = ctx.enter_context(nc.sbuf_tensor("ln_eps", [P, 1], F32))
    e.psum = ctx.enter_context(nc.psum_tensor("psum", [P, 8 * BANK], F32))
    return e


def stage_load(nc, env, x):
    with ExitStack() as ctx:
        x_loaded = env.ctx.enter_context(nc.semaphore("x_loaded"))
        consts = env.ctx.enter_context(nc.semaphore("consts"))
        block = ctx.enter_context(nc.Block())
        xv = x.rearrange("(t p) d -> p t d", p=P)

        @block.sync
        def _(sp):
            for q in range(4):
                sl = slice(q * NT // 4, (q + 1) * NT // 4)
                sp.dma_start(env.X[:, sl, :], xv[:, sl, :]).then_inc(x_loaded, 16)
            sp.wait_ge(x_loaded, 64)

        @block.gpsimd
        def _(pool):
            pool.memset(env.ident[:, :], 0.0).then_inc(consts, 1)
            pool.memset(env.ident_bf[:, :], 0.0).then_inc(consts, 1)
            pool.memset(env.ln_eps[:, :], LN_EPS).then_inc(consts, 1)
            pool.wait_ge(consts, 3)
            for m in (env.ident, env.ident_bf):
                pool.affine_select(out=m[:, :], in_=m[:, :], compare_op=ALU.not_equal, fill=1.0, base=0,
                                   pattern=[[-1, P]], channel_multiplier=1).then_inc(consts, 1)
            pool.wait_ge(consts, 5)


def stage_ln_stats(nc, env, name):
    with ExitStack() as ctx:
        stats = ctx.enter_context(nc.sbuf_tensor(f"{name}_stats", [P, NT, 6], F32))
        tmp = ctx.enter_context(nc.sbuf_tensor(f"{name}_tmp", [P, 4, NT], F32))
        stats_done = env.ctx.enter_context(nc.semaphore(f"{name}_stats_done"))
        step = env.ctx.enter_context(nc.semaphore(f"{name}_step"))
        var_done = env.ctx.enter_context(nc.semaphore(f"{name}_var_done"))
        std_done = env.ctx.enter_context(nc.semaphore(f"{name}_std_done"))
        block = ctx.enter_context(nc.Block())

        @block.vector
        def _(dve):
            with dve.Fori(0, NT) as t:
                nc.vector.bn_stats(stats[:, bass.ds(t, 1), :].rearrange("p a s -> p (a s)"),
                                   env.X[:, bass.ds(t, 1), :].rearrange("p a d -> p (a d)")).then_inc(stats_done, 1)
            dve.wait_ge(stats_done, NT)
            m0, v0, m1, v1 = (stats[:, :, i] for i in (1, 2, 4, 5))
            nc.vector.tensor_tensor(tmp[:, 0, :], m0, m1, ALU.add).then_inc(step, 1)
            nc.vector.tensor_tensor(tmp[:, 1, :], m0, m1, ALU.subtract).then_inc(step, 1)
            nc.vector.tensor_tensor(tmp[:, 2, :], v0, v1, ALU.add).then_inc(step, 1)
            dve.wait_ge(step, 3)
            nc.vector.tensor_scalar(env.mean[:, :], tmp[:, 0, :], 0.5, None, ALU.mult).then_inc(step, 1)
            nc.vector.tensor_tensor(tmp[:, 3, :], tmp[:, 1, :], tmp[:, 1, :], ALU.mult).then_inc(step, 1)
            dve.wait_ge(step, 5)
            nc.vector.tensor_scalar(tmp[:, 3, :], tmp[:, 3, :], D / 4.0, None, ALU.mult).then_inc(step, 1)
            dve.wait_ge(step, 6)
            nc.vector.tensor_tensor(tmp[:, 0, :], tmp[:, 2, :], tmp[:, 3, :], ALU.add).then_inc(var_done, 1)
            dve.wait_ge(std_done, 1)
            nc.vector.reciprocal(env.rstd[:, :], tmp[:, 1, :]).then_inc(step, 1)
            dve.wait_ge(step, 7)

        @block.scalar
        def _(act):
            act.wait_ge(var_done, 1)
            nc.scalar.activation(tmp[:, 1, :], tmp[:, 0, :], ACT.Sqrt, bias=env.ln_eps[:, 0:1],
                                 scale=1.0 / D).then_inc(std_done, 1)


E, R = 8, 4
NB_OUT = D + E + E * R


def stage_ffn(nc, env, name, w_cat, right_aug, out=None):
    ER = E * R
    RA = ER + 1
    NQ = NT // 4
    with ExitStack() as ctx:
        def sb(n, shape, dt=F32):
            return ctx.enter_context(nc.sbuf_tensor(f"{name}_{n}", shape, dt))

        def sem(n):
            return env.ctx.enter_context(nc.semaphore(f"{name}_{n}"))

        wc = sb("wc", [P, KC, NB_OUT])
        ra = sb("ra", [RA, D])
        rank = sb("rank", [P, E])
        xn = sb("xn", [P, 4, D])
        xnT = sb("xnT", [P, 4, D])
        raw = sb("raw", [P, NT, E + ER])
        prob, rest, hit, first, second = (sb(n, [P, NT, E]) for n in ("prob", "rest", "hit", "first", "second"))
        row = sb("row", [P, 4, NT])
        tl = sb("tl", [P, NT, RA])
        tlT = sb("tlT", [RA, 2, 4 * P])
        w_loaded, rank_done, ones_done = sem("w_loaded"), sem("rank_done"), sem("ones_done")
        xn_done, xT_done, xT_copied = sem("xn_done"), sem("xT_done"), sem("xT_copied")
        joint_done, base_added, raw_copied = sem("joint_done"), sem("base_added"), sem("raw_copied")
        step, shifted, exp_done, tl_done = sem("step"), sem("shifted"), sem("exp_done"), sem("tl_done")
        tlT_done, tlT_copied, lora_done = sem("tlT_done"), sem("tlT_copied"), sem("lora_done")
        x_added, stored = sem("x_added"), sem("stored")
        block = ctx.enter_context(nc.Block())

        def ps_xT(j):
            return env.psum[:, j % 2 * BANK:j % 2 * BANK + D]

        def ps_joint(j, a, b):
            return env.psum[:, (2 + j) * BANK + a:(2 + j) * BANK + b]

        def ps_tlT(j):
            return env.psum[0:RA, j * BANK:(j + 1) * BANK]

        def ps_lora(j, h):
            return env.psum[:, (2 + 2 * j + h) * BANK:(3 + 2 * j + h) * BANK]

        def tiles_of_X(t, n=1):
            return env.X[:, bass.ds(t, n), :].rearrange("p a d -> p (a d)")

        def over_quads(eng, body):
            for j in range(4):
                body(j, j, True, False)
            with eng.Fori(1, NQ - 1) as q:
                for j in range(4):
                    body(q * 4 + j, j, False, False)
            for j in range(4):
                body(NT - 4 + j, j, False, True)

        def over_quad_pairs(eng, body):
            body(0, True)
            with eng.Fori(1, NQ // 2) as i:
                body(i * 2, False)

        @block.sync
        def _(sp):
            sp.dma_start(wc[:, :, :], w_cat.rearrange("(c p) n -> p c n", p=P)).then_inc(w_loaded, 16)
            sp.dma_start(ra[:, :], right_aug).then_inc(w_loaded, 16)
            if out is not None:
                ov = out.rearrange("(t p) d -> p t d", p=P)
                for q in range(NQ):
                    sp.wait_ge(x_added, 2 * (q + 1))
                    sp.dma_start(ov[:, 4 * q:4 * q + 4, :], env.X[:, 4 * q:4 * q + 4, :]).then_inc(stored, 16)
                sp.wait_ge(stored, 16 * NQ)

        @block.gpsimd
        def _(pool):
            for j in range(E):
                pool.memset(rank[:, j:j + 1], float(E - j)).then_inc(rank_done, 1)
            pool.memset(tl[:, :, ER:RA], 1.0).then_inc(ones_done, 1)

        @block.vector
        def _(dve):
            def normalize(t, j, first_quad=False):
                if not first_quad:
                    dve.wait_ge(xT_done, t - 3)
                nc.vector.tensor_scalar(xn[:, j, :], tiles_of_X(t), env.mean[:, bass.ds(t, 1)],
                                        env.rstd[:, bass.ds(t, 1)], ALU.subtract, ALU.mult).then_inc(xn_done, 1)

            def base(t, j, first_quad, last_quad):
                dve.wait_ge(joint_done, t + 1)
                dve.wait_ge(raw_copied, t + 1)
                dve.wait_ge(xn_done, t + 1)
                nc.vector.tensor_tensor(tiles_of_X(t), ps_joint(j, 0, D), tiles_of_X(t), ALU.add).then_inc(base_added, 1)
                if not last_quad:
                    normalize(t + 4, j)

            for j in range(4):
                normalize(j, j, True)
            over_quads(dve, base)

            done = [0]

            def then(ins):
                done[0] += 1
                ins.then_inc(step, 1)
                dve.wait_ge(step, done[0])

            def of_row(i):
                return row[:, i, :].unsqueeze(2).to_broadcast([P, NT, E])

            ranks = rank[:, :].unsqueeze(1).to_broadcast([P, NT, E])
            logits = raw[:, :, 0:E]
            dve.wait_ge(raw_copied, NT)
            dve.wait_ge(rank_done, E)
            then(nc.vector.reduce_max(row[:, 0, :], logits, AX.X))
            nc.vector.tensor_tensor(prob[:, :, :], logits, of_row(0), ALU.subtract).then_inc(shifted, 1)
            dve.wait_ge(exp_done, 1)
            then(nc.vector.reduce_sum(row[:, 1, :], prob[:, :, :], AX.X))
            then(nc.vector.reciprocal(row[:, 1, :], row[:, 1, :]))
            then(nc.vector.tensor_tensor(prob[:, :, :], prob[:, :, :], of_row(1), ALU.mult))

            def best(p, one):
                then(nc.vector.reduce_max(row[:, 2, :], p[:, :, :], AX.X))
                then(nc.vector.tensor_tensor(hit[:, :, :], p[:, :, :], of_row(2), ALU.is_equal))
                then(nc.vector.tensor_tensor(hit[:, :, :], hit[:, :, :], ranks, ALU.mult))
                then(nc.vector.reduce_max(row[:, 3, :], hit[:, :, :], AX.X))
                then(nc.vector.tensor_tensor(one[:, :, :], hit[:, :, :], of_row(3), ALU.is_equal))

            best(prob, first)
            then(nc.vector.tensor_scalar(rest[:, :, :], first[:, :, :], -4.0, None, ALU.mult))
            then(nc.vector.tensor_tensor(rest[:, :, :], rest[:, :, :], prob[:, :, :], ALU.add))
            best(rest, second)
            then(nc.vector.tensor_tensor(first[:, :, :], first[:, :, :], second[:, :, :], ALU.add))
            then(nc.vector.tensor_tensor(first[:, :, :], first[:, :, :], prob[:, :, :], ALU.mult))
            nc.vector.tensor_tensor(tl[:, :, 0:ER].rearrange("p t (e r) -> p t e r", r=R),
                                    raw[:, :, E:E + ER].rearrange("p t (e r) -> p t e r", r=R),
                                    first[:, :, :].unsqueeze(3).to_broadcast([P, NT, E, R]),
                                    ALU.mult).then_inc(tl_done, 1)
            dve.wait_ge(base_added, NT)

            def add(q0, first_pair):
                for j in range(2):
                    for h in range(2):
                        n = (q0 + j) * 2 + h
                        dve.wait_ge(lora_done, n + 1)
                        xt = tiles_of_X(n * 2, 2)
                        nc.vector.tensor_tensor(xt, ps_lora(j, h), xt, ALU.add).then_inc(x_added, 1)

            over_quad_pairs(dve, add)
            dve.wait_ge(x_added, 2 * NQ)

        @block.scalar
        def _(act):
            nc.scalar.preload_act_table_set("exp_and_others")

            def transposed(t, j, first_quad=False):
                act.wait_ge(xT_done, t + 1)
                if not first_quad:
                    act.wait_ge(joint_done, t - 3)
                nc.scalar.activation(xnT[:, j, :], ps_xT(j), ACT.Copy).then_inc(xT_copied, 1)

            def raws(t, j, first_quad, last_quad):
                act.wait_ge(joint_done, t + 1)
                nc.scalar.activation(raw[:, bass.ds(t, 1), :].rearrange("p a n -> p (a n)"), ps_joint(j, D, NB_OUT),
                                     ACT.Copy).then_inc(raw_copied, 1)
                if not (last_quad and j >= 2):
                    transposed(t + 2, (j + 2) % 4, first_quad and j < 2)

            for j in range(2):
                transposed(j, j, True)
            over_quads(act, raws)
            act.wait_ge(shifted, 1)
            nc.scalar.activation(prob[:, :, :], prob[:, :, :], ACT.Exp).then_inc(exp_done, 1)

            def left(q0, first_pair):
                for j in range(2):
                    act.wait_ge(tlT_done, q0 + j + 1)
                    if not first_pair:
                        act.wait_ge(lora_done, (q0 + j - 1) * 2)
                    nc.scalar.activation(tlT[:, j, :], ps_tlT(j), ACT.Copy).then_inc(tlT_copied, 1)

            over_quad_pairs(act, left)

        @block.tensor
        def _(pe):
            pe.wait_ge(w_loaded, 32)

            def transpose_x(t, j):
                pe.wait_ge(xn_done, t + 1)
                for c in range(KC):
                    last = nc.tensor.transpose(ps_xT(j)[:, c * P:(c + 1) * P], xn[:, j, c * P:(c + 1) * P], env.ident[:, :])
                last.then_inc(xT_done, 1)

            def joint(t, j, first_quad, last_quad):
                pe.wait_ge(xT_copied, t + 1)
                if not first_quad:
                    pe.wait_ge(base_added, t - 3)
                    pe.wait_ge(raw_copied, t - 3)
                for c in range(KC):
                    last = nc.tensor.matmul(ps_joint(j, 0, NB_OUT), xnT[:, j, c * P:(c + 1) * P], wc[:, c, :],
                                            start=(c == 0), stop=(c == KC - 1))
                last.then_inc(joint_done, 1)
                if not (last_quad and j >= 2):
                    transpose_x(t + 2, (j + 2) % 4)

            for j in range(2):
                transpose_x(j, j)
            over_quads(pe, joint)
            pe.wait_ge(base_added, NT)
            pe.wait_ge(ones_done, 1)
            pe.wait_ge(tl_done, 1)

            def lora(q0, first_pair):
                for j in range(2):
                    if not first_pair:
                        pe.wait_ge(tlT_copied, q0 + j - 1)
                    for i in range(4):
                        last = nc.tensor.transpose(ps_tlT(j)[:, i * P:(i + 1) * P], tl[:, (q0 + j) * 4 + i, :],
                                                   env.ident[:, :])
                    last.then_inc(tlT_done, 1)
                for j in range(2):
                    pe.wait_ge(tlT_copied, q0 + j + 1)
                    for h in range(2):
                        if not first_pair:
                            pe.wait_ge(x_added, (q0 + j) * 2 + h - 3)
                        for i in range(2):
                            last = nc.tensor.matmul(ps_lora(j, h)[:, i * D:(i + 1) * D],
                                                    tlT[:, j, (2 * h + i) * P:(2 * h + i + 1) * P], ra[:, :],
                                                    start=True, stop=True, skip_group_check=True)
                        last.then_inc(lora_done, 1)

            for q0 in range(0, NQ, 2):
                lora(q0, q0 == 0)


HA, DH = 16, 64
PAIRS = HA // 2
IB = 256
NIB = SEQ // IB
SCALE = DH ** -0.5
NEG = -1e30


def stage_attn_a(nc, env, wqk, wv, wo, bo, slopes):
    UNITS = 2 * TB
    chunks, evacs = [], []
    for u in range(UNITS):
        n = (u // 2 + 1) * P
        chunks.append([(a, min(a + 2 * BANK, n)) for a in range(0, n, 2 * BANK)])
        evacs.append([(a, min(a + 4, u // 2 + 1)) for a in range(0, u // 2 + 1, 4)])
    chunk0 = [sum(len(c) for c in chunks[:u]) for u in range(UNITS + 1)]
    evac0 = [sum(len(c) for c in evacs[:u]) for u in range(UNITS + 1)]
    NCH, NEV = chunk0[UNITS], evac0[UNITS]
    LAG = 3
    ROWS = 4
    NV, NQK = 4, 16
    NPROJ = NV + NQK
    on_dve = [e % 3 == 2 for e in range(NEV)]

    def count(flags, upto):
        return sum(flags[:upto])

    n_dve = count(on_dve, NEV)
    n_act = NEV - n_dve
    av_step = {ib: 4 * (ib + 1) + LAG for ib in range(NIB)}
    op_step = {ib: 4 * (ib + 1) + LAG + 2 for ib in range(NIB)}
    STEPS = UNITS + LAG + 4

    with ExitStack() as ctx:
        def sb(n, shape, dt=F32):
            return ctx.enter_context(nc.sbuf_tensor(f"a_{n}", shape, dt))

        def sem(n):
            return env.ctx.enter_context(nc.semaphore(f"a_{n}"))

        xnT = sb("xnT", [P, KC, SEQ])
        wqk_sb = sb("wqk", [P, 2, 2, KC, 2, DH])
        wv_sb = sb("wv", [P, KC, 2 * DH])
        wo_sb = sb("wo", [P, D])
        bo_sb = sb("bo", [P, D])
        slope_sb = sb("slope", [P, HA])
        iota_j = sb("iota_j", [P, SEQ])
        bias = sb("bias", [P, 2, SEQ])
        mask = sb("mask", [P, P], BF16)
        q_st = sb("q_st", [P, 2, SEQ], F32R)
        k_hi = sb("k_hi", [P, 2, SEQ], F32R)
        k_lo = sb("k_lo", [P, 2, SEQ], F32R)
        v_sb = sb("v", [P, TB, 2 * DH])
        srow = sb("srow", [P, ROWS, SEQ])
        xn = srow[:, 0, 0:4 * D].rearrange("p (j d) -> p j d", d=D)
        pT = sb("pT", [P, 2, TB, IB])
        cmax = sb("cmax", [P, UNITS, 2])
        nmax = sb("nmax", [P, UNITS])
        zsum = sb("zsum", [P, UNITS])
        zinv = sb("zinv", [P, UNITS])
        zrep = sb("zrep", [P, 4, 2, DH])
        zT = sb("zT", [P, IB])
        oT = sb("oT", [P, 2, IB])

        consts, w_loaded, wo_loaded, mask_done = sem("consts"), sem("w_loaded"), sem("wo_loaded"), sem("mask_done")
        iota_done = sem("iota_done")
        xn_done, xT_done, xT_copied = sem("xn_done"), sem("xT_done"), sem("xT_copied")
        proj_done, v_copied, hi_done, lo_done = sem("proj_done"), sem("v_copied"), sem("hi_done"), sem("lo_done")
        bias_done = sem("bias_done")
        scores_done, max_done, nmax_done = sem("scores_done"), sem("max_done"), sem("nmax_done")
        exp_done, zinv_done, zrep_done = sem("exp_done"), sem("zinv_done"), sem("zrep_done")
        probT_done, act_evac, dve_evac = sem("probT_done"), sem("act_evac"), sem("dve_evac")
        zT_done, zT_copied, av_done, oT_done = sem("zT_done"), sem("zT_copied"), sem("av_done"), sem("oT_done")
        op_done, x_added = sem("op_done"), sem("x_added")
        passed = sem("passed")
        block = ctx.enter_context(nc.Block())

        PT_BANKS = (4, 5, 7)

        def bank(i, a=0, b=BANK):
            return env.psum[:, i * BANK + a:i * BANK + b]

        def ps_scores(c, width):
            return env.psum[:, (c % 2) * 2 * BANK:(c % 2) * 2 * BANK + width]

        def evacuate(eng, copy, u, g, dve_side):
            h, it = u % 2, u // 2
            il = it % 2
            for i, (a, z) in enumerate(evacs[u]):
                e = evac0[u] + i
                if on_dve[e] != dve_side:
                    continue
                eng.wait_ge(probT_done, g * NEV + e + 1)
                if it % 2 == 0 and i == 0 or (it % 2 == 0 and count(on_dve, e) == count(on_dve, evac0[u]) and dve_side):
                    if it >= 2:
                        eng.wait_ge(av_done, g * NIB + it // 2)
                    else:
                        eng.wait_ge(av_done, g * NIB)
                src = bank(PT_BANKS[e % 3], 0, (z - a) * P).rearrange("p (j i) -> p j i", i=P)
                copy(pT[:, h, a:z, il * P:(il + 1) * P], src).then_inc(dve_evac if dve_side else act_evac, 1)

        @block.sync
        def _(sp):
            sp.dma_start(bo_sb[:, :], bo.to_broadcast([P, D])).then_inc(consts, 16)
            sp.dma_start(slope_sb[:, :], slopes.to_broadcast([P, HA])).then_inc(consts, 16)
            with sp.Fori(0, BATCH) as b:
                with sp.Fori(0, PAIRS) as hp:
                    g = b * PAIRS + hp
                    sp.wait_ge(proj_done, g * NPROJ)
                    for h in range(2):
                        for c in range(2):
                            sp.dma_start(wqk_sb[:, h, :, :, c, :],
                                         wqk[bass.ds(hp * 2 + h, 1)].rearrange("a p t c d -> p (a t) c d")
                                         ).then_inc(w_loaded, 16)
                    sp.dma_start(wv_sb[:, :, :], wv[bass.ds(hp, 1)].rearrange("a p c d -> p (a c) d")).then_inc(w_loaded, 16)
                    sp.wait_ge(op_done, g * NIB)
                    sp.dma_start(wo_sb[:, :], wo[bass.ds(hp, 1)].rearrange("a p d -> p (a d)")).then_inc(wo_loaded, 16)

        @block.gpsimd
        def _(pool):
            pool.iota(iota_j[:, :], pattern=[[1, SEQ]], base=0, channel_multiplier=0,
                      allow_small_or_imprecise_dtypes=True).then_inc(iota_done, 1)
            pool.memset(mask[:, :], 0.0).then_inc(mask_done, 1)
            pool.wait_ge(mask_done, 1)
            pool.affine_select(out=mask[:, :], in_=mask[:, :], compare_op=ALU.is_ge, fill=NEG, base=0,
                               pattern=[[-1, P]], channel_multiplier=1).then_inc(mask_done, 1)

        @block.vector
        def _(dve):
            dve.wait_ge(consts, 32)
            dve.wait_ge(iota_done, 1)
            with dve.Fori(0, BATCH) as b:
                with dve.Fori(0, TB // 4) as quad:
                    for j in range(4):
                        t = b * TB + quad * 4 + j
                        dve.wait_ge(xT_done, (b * TB + quad * 4) * 1)
                        xt = env.X[:, bass.ds(t, 1), :].rearrange("p a d -> p (a d)")
                        nc.vector.tensor_scalar(xn[:, j, :], xt, env.mean[:, bass.ds(t, 1)],
                                                env.rstd[:, bass.ds(t, 1)], ALU.subtract, ALU.mult).then_inc(xn_done, 1)
                    for j in range(4):
                        t = b * TB + quad * 4 + j
                        xt = env.X[:, bass.ds(t, 1), :].rearrange("p a d -> p (a d)")
                        dve.wait_ge(xn_done, t + 1)
                        nc.vector.tensor_tensor(xt, xt, bo_sb[:, :], ALU.add).then_inc(x_added, 1)
                with dve.Fori(0, PAIRS) as hp:
                    g = b * PAIRS + hp
                    added = b * TB + TB + g * NIB
                    for h in range(2):
                        dve.wait_ge(max_done, g * NCH)
                        nc.vector.tensor_scalar(bias[:, h, :], iota_j[:, :], slope_sb[:, bass.ds(hp * 2 + h, 1)],
                                                -1.0 / SCALE, ALU.mult, ALU.mult).then_inc(bias_done, 1)
                    for v in range(NQK):
                        blk, h, t = v // 4, v // 2 % 2, v % 2
                        cols = slice(blk * BANK, (blk + 1) * BANK)
                        ps = bank((NV + v) % 4)
                        dve.wait_ge(hi_done, g * NQK + v + 1)
                        if t == 0:
                            nc.vector.tensor_tensor(q_st[DH:P, h, cols], ps[DH:P, :], q_st[DH:P, h, cols].bitcast(F32),
                                                    ALU.subtract).then_inc(lo_done, 1)
                        else:
                            nc.vector.tensor_tensor(k_lo[:, h, cols], ps, k_hi[:, h, cols].bitcast(F32),
                                                    ALU.subtract).then_inc(lo_done, 1)
                    dve.wait_ge(bias_done, (g + 1) * 2)
                    for s in range(STEPS):
                        u = s
                        if u < UNITS:
                            h, row = u % 2, u % ROWS
                            if u >= ROWS:
                                dve.wait_ge(probT_done, g * NEV + evac0[u - ROWS + 1])
                            else:
                                dve.wait_ge(probT_done, g * NEV)
                            for i, (a, z) in enumerate(chunks[u]):
                                dve.wait_ge(scores_done, g * NCH + chunk0[u] + i + 1)
                                dve.sem_inc(passed, 1)
                                nc.vector.tensor_tensor_reduce(
                                    out=srow[:, row, a:z], in0=ps_scores(chunk0[u] + i, z - a), in1=bias[:, h, a:z],
                                    scale=1.0, scalar=-3e38, op0=ALU.add, op1=ALU.max,
                                    accum_out=cmax[:, u, i:i + 1]).then_inc(max_done, 1)
                            dve.wait_ge(max_done, g * NCH + chunk0[u + 1])
                            if len(chunks[u]) == 1:
                                nc.vector.tensor_scalar(nmax[:, u:u + 1], cmax[:, u, 0:1], -SCALE, None,
                                                        ALU.mult).then_inc(nmax_done, 1)
                            else:
                                nc.vector.tensor_scalar(nmax[:, u:u + 1], cmax[:, u, 0:1], cmax[:, u, 1:2], -SCALE,
                                                        ALU.max, ALU.mult).then_inc(nmax_done, 1)
                        if 0 <= s - 2 < UNITS:
                            w = s - 2
                            dve.wait_ge(exp_done, g * UNITS + w + 1)
                            nc.vector.reciprocal(zinv[:, w:w + 1], zsum[:, w:w + 1]).then_inc(zinv_done, 1)
                            if w % 2:
                                dve.wait_ge(zinv_done, g * UNITS + w + 1)
                                dve.wait_ge(zT_done, g * NIB + max(w // 4 - 1, 0))
                                nc.vector.tensor_copy(zrep[:, w // 2 % 4, :, :],
                                                      zinv[:, w - 1:w + 1].unsqueeze(2).to_broadcast([P, 2, DH])
                                                      ).then_inc(zrep_done, 1)
                        for ib in range(NIB):
                            if av_step[ib] + 1 == s:
                                dve.wait_ge(av_done, g * NIB + ib + 1)
                                dve.wait_ge(zT_copied, g * NIB + ib + 1)
                                if ib >= 2:
                                    dve.wait_ge(op_done, g * NIB + ib - 1)
                                else:
                                    dve.wait_ge(op_done, g * NIB)
                                nc.vector.tensor_tensor(oT[:, ib % 2, :], bank(6, 0, IB), zT[:, :],
                                                        ALU.mult).then_inc(oT_done, 1)
                            if op_step[ib] + 1 == s:
                                dve.wait_ge(op_done, g * NIB + ib + 1)
                                dve.wait_ge(x_added, added + ib)
                                xt = env.X[:, bass.ds(b * TB + 2 * ib, 2), :].rearrange("p a d -> p (a d)")
                                nc.vector.tensor_tensor(xt, bank(6), xt, ALU.add).then_inc(x_added, 1)
                        if 0 <= s - LAG < UNITS:
                            evacuate(dve, nc.vector.tensor_copy, s - LAG, g, True)
                dve.wait_ge(x_added, (b + 1) * (TB + NIB * PAIRS))

        @block.scalar
        def _(act):
            nc.scalar.preload_act_table_set("exp_and_others")
            with act.Fori(0, BATCH) as b:
                with act.Fori(0, TB // 4) as quad:
                    for c in range(KC):
                        k = (b * (TB // 4) + quad) * KC + c
                        act.wait_ge(xT_done, (b * TB + quad * 4 + 4))
                        nc.scalar.activation(xnT[:, c, bass.ds(quad * BANK, BANK)], bank(4 + c), ACT.Copy
                                             ).then_inc(xT_copied, 1)
                with act.Fori(0, PAIRS) as hp:
                    g = b * PAIRS + hp
                    act.wait_ge(av_done, g * NIB)
                    for v in range(NV):
                        act.wait_ge(proj_done, g * NPROJ + v + 1)
                        nc.scalar.activation(v_sb[:, 4 * v:4 * v + 4, :],
                                             bank(v).rearrange("p (t d) -> p t d", t=4), ACT.Copy).then_inc(v_copied, 1)
                    act.wait_ge(scores_done, g * NCH)
                    for v in range(NQK):
                        blk, h, t = v // 4, v // 2 % 2, v % 2
                        cols = slice(blk * BANK, (blk + 1) * BANK)
                        act.wait_ge(proj_done, g * NPROJ + NV + v + 1)
                        nc.scalar.activation((k_hi if t else q_st)[:, h, cols], bank((NV + v) % 4), ACT.Copy
                                             ).then_inc(hi_done, 1)
                    for s in range(STEPS):
                        if 0 <= s - 1 < UNITS:
                            u = s - 1
                            act.wait_ge(nmax_done, g * UNITS + u + 1)
                            n = (u // 2 + 1) * P
                            nc.scalar.activation(srow[:, u % ROWS, 0:n], srow[:, u % ROWS, 0:n], ACT.Exp,
                                                 bias=nmax[:, u:u + 1], scale=SCALE,
                                                 accum_out=zsum[:, u:u + 1]).then_inc(exp_done, 1)
                        for ib in range(NIB):
                            if av_step[ib] == s:
                                act.wait_ge(av_done, g * NIB + ib + 1)
                                act.wait_ge(oT_done, g * NIB + ib)
                                nc.scalar.activation(zT[:, :], bank(6, IB, BANK), ACT.Copy).then_inc(zT_copied, 1)
                        if 0 <= s - LAG < UNITS:
                            evacuate(act, lambda o, i: nc.scalar.activation(o, i, ACT.Copy), s - LAG, g, False)

        @block.tensor
        def _(pe):
            pe.wait_ge(mask_done, 2)
            with pe.Fori(0, BATCH) as b:
                with pe.Fori(0, TB // 4) as quad:
                    pe.wait_ge(xT_copied, (b * (TB // 4) + quad) * KC)
                    for j in range(4):
                        pe.wait_ge(xn_done, b * TB + quad * 4 + j + 1)
                        for c in range(KC):
                            last = nc.tensor.transpose(bank(4 + c, j * P, (j + 1) * P), xn[:, j, c * P:(c + 1) * P],
                                                       env.ident[:, :])
                        last.then_inc(xT_done, 1)
                pe.wait_ge(xT_copied, (b + 1) * (TB // 4) * KC)
                pe.sem_inc(passed, 1)
                with pe.Fori(0, PAIRS) as hp:
                    g = b * PAIRS + hp
                    pe.wait_ge(w_loaded, (g + 1) * 16 * 5)
                    pe.wait_ge(max_done, g * NCH)
                    for v in range(NV):
                        for t in range(4):
                            for c in range(KC):
                                last = nc.tensor.matmul(bank(v, t * P, (t + 1) * P),
                                                        xnT[:, c, (4 * v + t) * P:(4 * v + t + 1) * P], wv_sb[:, c, :],
                                                        start=(c == 0), stop=(c == KC - 1))
                        last.then_inc(proj_done, 1)
                    for v in range(NQK):
                        blk, h, t = v // 4, v // 2 % 2, v % 2
                        if v < 4:
                            pe.wait_ge(v_copied, g * NV + v + 1)
                        else:
                            pe.wait_ge(lo_done, g * NQK + v - 3)
                        for c in range(KC):
                            last = nc.tensor.matmul(bank((NV + v) % 4),
                                                    wqk_sb[:, h, t, c, :, :].rearrange("p a d -> p (a d)"),
                                                    xnT[:, c, blk * BANK:(blk + 1) * BANK],
                                                    start=(c == 0), stop=(c == KC - 1))
                        last.then_inc(proj_done, 1)
                    pe.wait_ge(lo_done, (g + 1) * NQK)

                    def scores(u):
                        it, h = u // 2, u % 2
                        rows = slice(it * P, (it + 1) * P)
                        for i, (a, z) in enumerate(chunks[u]):
                            c = chunk0[u] + i
                            if c >= 2:
                                pe.wait_ge(max_done, g * NCH + c - 1)
                            for s0 in range(a, z, BANK):
                                s1 = min(s0 + BANK, z)
                                o = ps_scores(c, 2 * BANK)[:, s0 - a:s1 - a]
                                last_one = s1 == (it + 1) * P
                                nc.tensor.matmul(o, q_st[:, h, rows], k_hi[:, h, s0:s1], start=True, stop=False)
                                last = nc.tensor.matmul(o, q_st[:, h, rows], k_lo[:, h, s0:s1], start=False,
                                                        stop=not last_one)
                                if last_one:
                                    last = nc.tensor.matmul(o[:, s1 - s0 - P:s1 - s0], env.ident_bf[:, :], mask[:, :],
                                                            start=False, stop=True)
                            last.then_inc(scores_done, 1)

                    def transposes(u):
                        pe.wait_ge(exp_done, g * UNITS + u + 1)
                        for i, (a, z) in enumerate(evacs[u]):
                            e = evac0[u] + i
                            p = e - 3
                            if p >= 0:
                                if on_dve[p]:
                                    pe.wait_ge(dve_evac, g * n_dve + count(on_dve, p + 1))
                                else:
                                    pe.wait_ge(act_evac, g * n_act + p + 1 - count(on_dve, p + 1))
                            else:
                                pe.wait_ge(dve_evac, g * n_dve)
                                pe.wait_ge(act_evac, g * n_act)
                            for jt in range(a, z):
                                last = nc.tensor.transpose(bank(PT_BANKS[e % 3], (jt - a) * P, (jt - a + 1) * P),
                                                           srow[:, u % ROWS, jt * P:(jt + 1) * P], env.ident[:, :])
                            last.then_inc(probT_done, 1)

                    def product_with_v(ib):
                        e = evac0[4 * (ib + 1)]
                        pe.wait_ge(zrep_done, g * TB + 2 * (ib + 1))
                        pe.wait_ge(x_added, b * TB + TB + g * NIB + ib)
                        for i in range(2):
                            last = nc.tensor.matmul(bank(6, IB + i * P, IB + (i + 1) * P),
                                                    zrep[:, (2 * ib + i) % 4, :, :].rearrange("p h d -> p (h d)"),
                                                    env.ident[:, :], start=(i == 0), stop=True, skip_group_check=True)
                        last.then_inc(zT_done, 1)
                        pe.wait_ge(dve_evac, g * n_dve + count(on_dve, e))
                        pe.wait_ge(act_evac, g * n_act + e - count(on_dve, e))
                        for jt in range(2 * ib + 2):
                            lo = P if jt == 2 * ib + 1 else 0
                            for h in range(2):
                                last = nc.tensor.matmul(bank(6, lo, IB)[h * DH:(h + 1) * DH, :],
                                                        v_sb[:, jt, h * DH:(h + 1) * DH], pT[:, h, jt, lo:IB],
                                                        start=(jt == 0), stop=(jt == 2 * ib + 1), skip_group_check=True)
                        last.then_inc(av_done, 1)

                    def out_projection(ib):
                        if ib == 0:
                            pe.wait_ge(wo_loaded, (g + 1) * 16)
                        pe.wait_ge(oT_done, g * NIB + ib + 1)
                        for i in range(2):
                            last = nc.tensor.matmul(bank(6, i * IB, (i + 1) * IB),
                                                    oT[:, ib % 2, i * P:(i + 1) * P], wo_sb[:, :], start=True, stop=True,
                                                    skip_group_check=True)
                        last.then_inc(op_done, 1)

                    for s in range(STEPS):
                        if s < UNITS:
                            scores(s)
                        for ib in range(NIB):
                            if av_step[ib] == s:
                                product_with_v(ib)
                            if op_step[ib] == s:
                                out_projection(ib)
                        if 0 <= s - LAG < UNITS:
                            transposes(s - LAG)


HB, DB = 16, 16
GUARD = 1e-5
FLOOR = 1e-12
AUG = DB + 2
SPLITS = 7
Q_PARTS, K_PARTS = "hmlhmhl", "hmlmhlh"
KST = SPLITS * AUG
COLS = SEQ
NCHK = TB
HALF = COLS // 2
A_RING, Y_RING = 4, 8
BATCHED = 4
SQUARES = "PAPDPAPDPAPDPAPD"
D_LAG = A_RING - 1
MAX_SHIFT = 80.0
MAX_DIST = 14.4


def stage_attn_b(nc, env, w_qkv, w_o, scalars, ra_scratch, x_scratch):
    with ExitStack() as ctx:
        def sb(n, shape, dt=F32):
            return ctx.enter_context(nc.sbuf_tensor(f"b_{n}", shape, dt))

        def sem(n):
            return env.ctx.enter_context(nc.semaphore(f"b_{n}"))

        tok = sb("tok", [P, 3, TB, D])
        y_ring = sb("y_ring", [P, Y_RING // 2, COLS])
        x_ring = env.X[:, :, :].rearrange("p t d -> p (t d)").rearrange("p (s n) -> p s n", n=COLS)
        a_ring = sb("a_ring", [P, A_RING, COLS])
        xnT = y_ring[:, 0:KC, :]
        xn = y_ring[:, 2, :].rearrange("p (j d) -> p j d", d=D)[:, 0:4, :]
        w_in = y_ring[:, 3, 0:KC * 3 * D].rearrange("p (c n) -> p c n", c=KC)
        sq = a_ring[:, 0, 0:2 * 3 * D].rearrange("p (j n) -> p j n", j=2)
        osq = y_ring[:, 0:2, :].rearrange("p a n -> p (a n)")
        oT = y_ring[:, 2, 0:2 * D].rearrange("p (j n) -> p j n", j=2)
        wo_sb = y_ring[:, 3, 0:KC * D].rearrange("p (c n) -> p c n", c=KC)
        ra_rep = sb("ra_rep", [P, 2, SEQ])
        qT = sb("qT", [KST, 2, SEQ], BF16)
        kT = sb("kT", [KST, 2, SEQ], BF16)
        v_aug = sb("v_aug", [P, 2, TB, 32])
        cap = sb("cap", [P, 2, TB])
        aug = sb("aug", [P, 2, TB, AUG])
        stack = sb("stack", [P, 2, TB, SPLITS, AUG], BF16)
        arr = sb("arr", [P, 4, TB * HB])
        o_sb = sb("o_sb", [P, BANK])
        zinv = sb("zinv", [P, TB])
        sc = sb("sc", [P, 24])
        NS_Q, E_K, EN_K, CAP_K = range(4)
        tmp = a_ring[:, 0, :].rearrange("p (i n) -> p i n", n=TB * HB)
        nsq = a_ring[:, 1, 0:3 * TB * HB].rearrange("p (i n) -> p i n", n=TB * HB)
        ons = a_ring[:, 2, 0:3 * TB * HB].rearrange("p (i n) -> p i n", n=TB * HB)
        raT = a_ring[:, 3, 0:2 * P].rearrange("p (c k) -> p c k", c=2)

        names = ("scal_loaded scal chain w_loaded wo_loaded zeroed xn_done xT_done xT_copied proj_done tok_copied "
                 "sq_done nsq_done root_all x_all th_all ra_done raT_done raT_copied ra_stored ra_loaded0 ra_loaded1 "
                 "pool_step stack_done grpT_done grp_copied "
                 "x_saved x_back v_ready scores_done scores_read a_ready sq_A sq_D sq_P root_done sum_done ln_done w_done av_done "
                 "o_copied oT_done o_done osq_done osum_done oroot_done o_scaled loT_done loT_copied out_done "
                 "x_added gz_done arr_freed passed").split()
        S = {n: sem(n) for n in names}
        block = ctx.enter_context(nc.Block())

        def bank(i, a=0, b=BANK):
            return env.psum[:, i * BANK + a:i * BANK + b]

        def half_ps(j):
            return env.psum[:, j * 2 * BANK:(j + 1) * 2 * BANK]

        (LOGC, BETA, C, SC, NEG_S, SHIFT, XMAX, ONE, MINUS1, C2, NEG_C) = range(11)

        def col(i, n=1):
            return sc[:, i:i + n]

        def slot(ring, k):
            return k % ring

        def y_slot(k):
            s = k % Y_RING
            return y_ring[:, s, :] if s < Y_RING // 2 else x_ring[:, s - Y_RING // 2, :]

        def av(n):
            return n + Y_RING

        def summed(n):
            return n + A_RING

        def squared(g, k):
            return g * SQUARES.count(SQUARES[k]) + SQUARES[:k].count(SQUARES[k])

        def square_by(eng, engine, name, g, k):
            if SQUARES[k] != name:
                return
            eng.wait_ge(S["a_ready"], g * NCHK + k + 1)
            eng.wait_ge(S["av_done"], g * NCHK + k + 1)
            a = a_ring[:, slot(A_RING, k), :]
            engine.tensor_tensor(y_slot(k), a, a, ALU.mult).then_inc(S["sq_" + name], 1)

        PREP = 20

        def prep(eng, engine, b, h, j, squares=False):
            g = b * HB + h
            todo = [k for k in range(NCHK) if SQUARES[k] == "P"] if squares else []
            early = [k for k in todo if k < NCHK // 2 - 1]
            every = PREP // (len(early) + 1)
            n = [0]

            def step(ins):
                n[0] += 1
                ins.then_inc(S["pool_step"], 1)
                if todo and todo[0] in early and n[0] % every == 0:
                    square_by(eng, engine, "P", g - 1, todo.pop(0))

            def sync():
                eng.wait_ge(S["pool_step"], g * PREP + n[0])
                eng.sem_inc(S["passed"], 1)

            def of(i):
                return arr[:, i, :].rearrange("p (t h) -> p t h", h=HB)[:, :, bass.ds(h, 1)]

            def toks(i):
                return tok[:, i, :, :].rearrange("p t (h d) -> p t h d", d=DB)[:, :, bass.ds(h, 1), :].rearrange(
                    "p t a d -> p t (a d)")

            if not (isinstance(h, int) and h < 2):
                eng.wait_ge(S["scores_read"], (g - 1) * 2 * NCHK)
                eng.sem_inc(S["passed"], 1)
            step(engine.tensor_copy(cap[:, j, :].unsqueeze(2), of(CAP_K)))
            step(engine.tensor_copy(aug[:, 0, :, 0:DB], toks(0)))
            step(engine.tensor_copy(aug[:, 0, :, DB:DB + 1], of(NS_Q)))
            step(engine.memset(aug[:, 0, :, DB + 1:AUG], 1.0))
            step(engine.tensor_copy(aug[:, 1, :, 0:DB], toks(1)))
            step(engine.tensor_copy(aug[:, 1, :, DB:DB + 1], of(E_K)))
            step(engine.tensor_copy(aug[:, 1, :, DB + 1:AUG], of(EN_K)))
            sync()
            eng.wait_ge(S["grpT_done"], g * 4)
            eng.sem_inc(S["passed"], 1)
            a2 = aug[:, :, :, :].rearrange("p a t d -> p (a t) d")
            s2 = stack[:, :, :, :, :].rearrange("p a t s d -> p (a t) s d")
            for i in range(3):
                step(engine.tensor_copy(s2[:, :, i, :], a2))
                sync()
                if i < 2:
                    step(engine.tensor_tensor(a2, a2, s2[:, :, i, :], ALU.subtract))
                    sync()
            for i, order in enumerate((Q_PARTS, K_PARTS)):
                for n_s in range(3, SPLITS):
                    step(engine.tensor_copy(stack[:, i, :, n_s, :], stack[:, i, :, "hml".index(order[n_s]), :]))
            sync()
            assert n[0] == PREP, n[0]
            eng.sem_inc(S["stack_done"], 1)
            while todo:
                square_by(eng, engine, "P", g - 1, todo.pop(0))
            if not (isinstance(h, int) and h < 2):
                eng.wait_ge(S["av_done"], av((g - 1) * NCHK))
                eng.sem_inc(S["passed"], 1)
            engine.tensor_copy(v_aug[:, j, :, 0:DB], toks(2)).then_inc(S["v_ready"], 1)

        @block.sync
        def _(sp):
            sp.dma_start(sc[:, LOGC:BETA + 1], scalars.to_broadcast([P, 2])).then_inc(S["scal_loaded"], 16)
            with sp.Fori(0, BATCH) as b:
                sp.wait_ge(S["x_added"], b * TB)
                sp.dma_start(w_in, w_qkv.rearrange("(c p) n -> p c n", p=P)).then_inc(S["w_loaded"], 16)
                xs = x_scratch.rearrange("(t p) d -> p t d", p=P)
                for q in range(4):
                    ts = slice(q * NT // 4, (q + 1) * NT // 4)
                    sp.dma_start(xs[:, ts, :], env.X[:, ts, :]).then_inc(S["x_saved"], 16)
                sp.wait_ge(S["raT_copied"], b + 1)
                sp.dma_start(ra_scratch[bass.ds(b, 1)].rearrange("a (c p) k -> p (a c) k", p=P), raT
                             ).then_inc(S["ra_stored"], 16)
                sp.wait_ge(S["ra_stored"], (b + 1) * 16)

                def load_ra(h, j):
                    g = b * HB + h
                    if not (isinstance(h, int) and h < 2):
                        sp.wait_ge(S["scores_read"], (g - 1) * 2 * NCHK)
                    else:
                        sp.wait_ge(S["scores_read"], b * HB * 2 * NCHK)
                    src = ra_scratch[bass.ds(b, 1)].rearrange("a (t h) k -> (a h) t k", h=HB)[bass.ds(h, 1)]
                    sp.dma_start(ra_rep[:, j, :].rearrange("p (t k) -> p t k", k=P), src.to_broadcast([P, TB, P])
                                 ).then_inc(S[f"ra_loaded{j}"], 16)

                load_ra(0, 0)
                load_ra(1, 1)
                with sp.Fori(0, HB // 2 - 1) as i:
                    load_ra(i * 2 + 2, 0)
                    load_ra(i * 2 + 3, 1)
                sp.wait_ge(S["av_done"], av((b + 1) * HB * NCHK))
                sp.dma_start(wo_sb, w_o.rearrange("(c p) n -> p c n", p=P)).then_inc(S["wo_loaded"], 16)
                sp.wait_ge(S["x_saved"], (b + 1) * 64)
                for q in range(4):
                    ts = slice(q * NT // 4, (q + 1) * NT // 4)
                    sp.dma_start(env.X[:, ts, :], xs[:, ts, :]).then_inc(S["x_back"], 16)
                sp.wait_ge(S["x_back"], (b + 1) * 64)
                sp.sem_inc(S["passed"], 1)

        @block.gpsimd
        def _(pool):
            count = [0]
            nc.gpsimd.memset(v_aug[:, :, :, :], 0.0).then_inc(S["zeroed"], 1)
            pool.wait_ge(S["zeroed"], 1)
            nc.gpsimd.memset(v_aug[:, :, :, DB:DB + 1], 1.0).then_inc(S["zeroed"], 1)
            pool.wait_ge(S["zeroed"], 2)
            with pool.Fori(0, BATCH) as b:
                pool.wait_ge(S["v_ready"], b * HB + 1)
                pool.wait_ge(S["x_saved"], (b + 1) * 64)
                pool.sem_inc(S["passed"], 1)
                prep(pool, nc.gpsimd, b, 1, 1, squares=True)
                with pool.Fori(0, HB // 2 - 1) as i:
                    prep(pool, nc.gpsimd, b, i * 2 + 2, 0, squares=True)
                    prep(pool, nc.gpsimd, b, i * 2 + 3, 1, squares=True)
                for k in range(NCHK):
                    square_by(pool, nc.gpsimd, "P", b * HB + HB - 1, k)

        @block.vector
        def _(dve):
            n_chain = [0]

            def link(ins):
                n_chain[0] += 1
                ins.then_inc(S["chain"], 1)
                dve.wait_ge(S["chain"], n_chain[0])

            T = 11
            dve.sem_inc(S["sum_done"], A_RING)
            dve.wait_ge(S["scal_loaded"], 16)
            link(nc.vector.memset(col(ONE), 1.0))
            link(nc.vector.memset(col(MINUS1), -1.0))
            link(nc.vector.tensor_scalar(col(T, 2), col(LOGC, 2), -1.0, None, ALU.mult))
            link(nc.vector.tensor_tensor(col(T, 2), col(T, 2), col(LOGC, 2), ALU.min))
            nc.vector.tensor_copy(col(T, 2), col(T, 2)).then_inc(S["gz_done"], 1)
            dve.wait_ge(S["scal"], 2)
            link(nc.vector.tensor_scalar(col(T, 2), col(T + 2, 2), 1.0, -1.0, ALU.add, ALU.add))
            link(nc.vector.tensor_scalar(col(T + 6, 2), col(T, 2), 0.0, None, ALU.is_equal))
            link(nc.vector.tensor_tensor(col(T, 2), col(T, 2), col(T + 6, 2), ALU.add))
            link(nc.vector.reciprocal(col(T, 2), col(T, 2)))
            link(nc.vector.tensor_tensor(col(T, 2), col(T, 2), col(T + 4, 2), ALU.mult))
            link(nc.vector.tensor_tensor(col(T, 2), col(T, 2), col(T + 6, 2), ALU.add))
            link(nc.vector.tensor_tensor(col(T, 2), col(T, 2), col(T + 2, 2), ALU.mult))
            link(nc.vector.tensor_scalar(col(T + 4, 2), col(LOGC, 2), 0.0, None, ALU.max))
            link(nc.vector.tensor_tensor(col(T, 2), col(T, 2), col(T + 4, 2), ALU.add))
            link(nc.vector.tensor_copy(col(C), col(T)))
            link(nc.vector.tensor_scalar(col(C2), col(T), 2.0, None, ALU.mult))
            link(nc.vector.tensor_scalar(col(NEG_C), col(T), -1.0, None, ALU.mult))
            nc.vector.tensor_copy(col(T + 8), col(T)).then_inc(S["gz_done"], 1)
            dve.wait_ge(S["scal"], 3)
            link(nc.vector.reciprocal(col(T + 2), col(SC)))
            link(nc.vector.tensor_tensor(col(T + 3), col(T + 1), col(T + 2), ALU.mult))
            link(nc.vector.tensor_scalar(col(NEG_S), col(T + 3), -1.0, None, ALU.mult))
            link(nc.vector.tensor_scalar(col(SHIFT), col(T + 3), MAX_DIST / 2, MAX_SHIFT, ALU.mult, ALU.min))
            link(nc.vector.tensor_scalar(col(T + 4), col(SC), GUARD, None, ALU.mult))
            link(nc.vector.reciprocal(col(T + 5), col(T + 4)))
            link(nc.vector.tensor_scalar(col(T + 6), col(T + 4), -1.0, 2.0, ALU.mult, ALU.add))
            link(nc.vector.tensor_tensor(col(T + 6), col(T + 6), col(T + 5), ALU.mult))
            nc.vector.tensor_copy(col(T + 7), col(T + 6)).then_inc(S["gz_done"], 1)
            dve.wait_ge(S["scal"], 4)
            link(nc.vector.tensor_scalar(col(XMAX), col(T + 9), 0.5, None, ALU.mult))
            n0 = n_chain[0]
            FACTORS = 24
            base = [None, 0]

            def chained(ins):
                base[1] += 1
                ins.then_inc(S["chain"], 1)
                dve.wait_ge(S["chain"], base[0] + base[1])

            def t3(x):
                return x.rearrange("p t (h d) -> p t h d", d=DB)

            with dve.Fori(0, BATCH) as b:
                base[0], base[1] = b * FACTORS + n0, 0
                dve.wait_ge(S["x_added"], b * TB)
                def normalize(t):
                    if t >= 4:
                        dve.wait_ge(S["xT_done"], b * TB + t - 3)
                    nc.vector.tensor_scalar(xn[:, t % 4, :], env.X[:, bass.ds(b * TB + t, 1), :].rearrange("p a d -> p (a d)"),
                                            env.mean[:, bass.ds(b * TB + t, 1)], env.rstd[:, bass.ds(b * TB + t, 1)],
                                            ALU.subtract, ALU.mult).then_inc(S["xn_done"], 1)
                nh = nsq.rearrange("p a (t h) -> p a t h", h=HB)

                def square_norms(t):
                    dve.wait_ge(S["sq_done"], b * TB + t + 1)
                    nc.vector.reduce_sum(nh[:, :, t, :], sq[:, t % 2, :].rearrange("p (a h d) -> p a h d", a=3, d=DB),
                                         AX.X).then_inc(S["nsq_done"], 1)

                for t in range(TB + 4):
                    if t < TB:
                        normalize(t)
                    if t % 4 == 3 and t >= 7:
                        for m in range(t - 7, t - 3):
                            square_norms(m)
                dve.wait_ge(S["root_all"], b + 1)
                x2, f2, n2 = tmp[:, 0:2, :], tmp[:, 3:5, :], tmp[:, 5:7, :]
                chained(nc.vector.tensor_scalar(x2, x2, GUARD, col(SC), ALU.max, ALU.mult))
                nc.vector.tensor_scalar(tmp[:, 2, :], tmp[:, 2, :], col(SC), 1e-30, ALU.mult, ALU.max).then_inc(S["x_all"], 1)
                dve.wait_ge(S["th_all"], b + 1)
                chained(nc.vector.reciprocal(x2, x2))
                chained(nc.vector.tensor_tensor(f2, f2, x2, ALU.mult))
                chained(nc.vector.tensor_tensor(n2, f2, f2, ALU.mult))
                chained(nc.vector.tensor_tensor(n2, n2, nsq[:, 0:2, :], ALU.mult))
                nc.vector.tensor_copy(arr[:, NS_Q, :], n2[:, 0, :])
                chained(nc.vector.tensor_scalar(x2, n2, col(NEG_C), 1.0, ALU.mult, ALU.add))
                chained(nc.vector.tensor_scalar(x2, x2, FLOOR, None, ALU.max))
                nc.vector.tensor_scalar(arr[:, CAP_K, :], x2[:, 1, :], 1.0 / GUARD, None, ALU.mult)
                chained(nc.vector.reciprocal(tmp[:, 7, :], x2[:, 1, :]))
                nc.vector.reciprocal(ons[:, 2, :], x2[:, 0, :]).then_inc(S["ra_done"], 1)
                chained(nc.vector.tensor_scalar(arr[:, E_K, :], tmp[:, 7, :], col(C2), None, ALU.mult))
                nc.vector.tensor_tensor(arr[:, EN_K, :], n2[:, 1, :], arr[:, E_K, :], ALU.mult)
                chained(nc.vector.tensor_tensor(f2[:, 1, :], f2[:, 1, :], arr[:, E_K, :], ALU.mult))
                chained(nc.vector.tensor_scalar(f2[:, 1, :], f2[:, 1, :], -2.0, None, ALU.mult))
                chained(nc.vector.reciprocal(tmp[:, 2, :], tmp[:, 2, :]))
                chained(nc.vector.tensor_scalar(tmp[:, 2, :], tmp[:, 2, :], col(XMAX), 1.0, ALU.mult, ALU.min))
                for i, f in enumerate((3, 4, 2)):
                    dst = tok[:, i, :, :].rearrange("p t n -> p (t n)").rearrange("p (n d) -> p n d", d=DB)
                    chained(nc.vector.tensor_tensor(dst, dst, tmp[:, f, :].unsqueeze(2).to_broadcast([P, TB * HB, DB]),
                                                    ALU.mult))
                dve.wait_ge(S["zeroed"], 2)
                dve.wait_ge(S["av_done"], av(b * HB * NCHK))
                prep(dve, nc.vector, b, 0, 0)

                def root_sum(g, k):
                    n = g * NCHK + k
                    dve.wait_ge(S["root_done"], n + 1)
                    kk = k % NCHK
                    y = y_slot(kk)
                    nc.vector.tensor_tensor(y, a_ring[:, slot(A_RING, kk), :], y, ALU.add).then_inc(S["sum_done"], 1)

                def argument(g, k, j):
                    a = a_ring[:, slot(A_RING, k), :]
                    dve.wait_ge(S["sum_done"], g * NCHK + k + 1)
                    for s in range(2):
                        dve.wait_ge(S["scores_done"], g * 2 * NCHK + 2 * k + s + 1)
                        nc.vector.scalar_tensor_tensor(out=a[:, s * HALF:(s + 1) * HALF],
                                                       in0=ra_rep[:, j, s * HALF:(s + 1) * HALF], scalar=cap[:, j, k:k + 1],
                                                       in1=half_ps(s), op0=ALU.min, op1=ALU.mult).then_inc(S["scores_read"], 1)

                def clamp(g, k):
                    a = a_ring[:, slot(A_RING, k), :]
                    dve.wait_ge(S["scores_read"], g * 2 * NCHK + 2 * k + 2)
                    nc.vector.tensor_scalar(a, a, 1.0, 1.0 + GUARD, ALU.add, ALU.max).then_inc(S["a_ready"], 1)

                def group_copied(g, i, j):
                    dve.wait_ge(S["grpT_done"], g * 4 + i + 1)
                    dst = (qT, kT)[i // 2][:, j, (i % 2) * 1024:(i % 2 + 1) * 1024]
                    nc.vector.tensor_copy(dst, bank(6 + (i + 1) % 2).bitcast(BF16)[0:KST, :]).then_inc(S["grp_copied"], 1)

                def out_copy(g):
                    dve.wait_ge(S["av_done"], av((g + 1) * NCHK))
                    dve.wait_ge(S["oT_done"], g)
                    nc.vector.tensor_copy(o_sb[:, :], out_bank(g_par)).then_inc(S["o_copied"], 1)

                def out_scale(g, h):
                    dve.wait_ge(S["oT_done"], g + 1)
                    o = bank(6).rearrange("p (c i d) -> p i c d", c=4, i=4)
                    z = zinv[:, :].rearrange("p (i c) -> p i c", c=4)
                    nc.vector.reciprocal(z.unsqueeze(3), o[:, :, :, DB:DB + 1]).then_inc(S["arr_freed"], 1)
                    dve.wait_ge(S["arr_freed"], g + 1)
                    for i in range(4):
                        dst = t3(tok[:, 0, 4 * i:4 * i + 4, :])[:, :, bass.ds(h, 1), :].rearrange("p t a d -> p t (a d)")
                        last = nc.vector.tensor_tensor(dst, o[:, i, :, 0:DB],
                                                       z[:, i, :].unsqueeze(2).to_broadcast([P, 4, DB]), ALU.mult)
                        last.then_inc(S["o_done"], 1)

                def out_bank(par):
                    return bank(4 + par)

                for i in range(4):
                    group_copied(b * HB, i, 0)
                dve.wait_ge(S["grp_copied"], b * HB * 4 + 4)

                def head(h, j, first, last):
                    nonlocal g_par
                    g = b * HB + h
                    dve.wait_ge(S[f"ra_loaded{j}"], (g - j) * 8 + 16)
                    dve.wait_ge(S["pool_step"], (g + 1) * PREP)
                    for k in range(NCHK):
                        argument(g, k, j)
                        if k % BATCHED == BATCHED - 1:
                            clamp(g, k)
                            for m in range(k + 1 - BATCHED, k + 1):
                                square_by(dve, nc.vector, "D", g, m)
                            root_sum(g, k - D_LAG)
                        else:
                            if k >= D_LAG or not first:
                                root_sum(g, k - D_LAG)
                            clamp(g, k)
                        if not first and k == 9:
                            g_par = 1 - j
                            out_copy(g - 1)
                        if not first and k == 11:
                            out_scale(g - 1, h - 1)
                        if not last and 11 <= k < 15:
                            group_copied(g + 1, k - 11, 1 - j)

                g_par = 0
                dve.wait_ge(S["x_saved"], (b + 1) * 64)
                head(0, 0, True, False)
                with dve.Fori(0, HB // 2 - 1) as i:
                    head(i * 2 + 1, 1, False, False)
                    head(i * 2 + 2, 0, False, False)
                head(HB - 1, 1, False, True)
                g = b * HB + HB
                for k in range(NCHK - D_LAG, NCHK):
                    root_sum(g, k - NCHK)
                g_par = 1
                out_copy(g - 1)
                out_scale(g - 1, HB - 1)
                dve.wait_ge(S["o_done"], g * 4)
                o_all = tok[:, 0, :, :].rearrange("p t n -> p (t n)")
                dve.wait_ge(S["av_done"], av(g * NCHK))
                nc.vector.tensor_tensor(osq, o_all, o_all, ALU.mult).then_inc(S["osq_done"], 1)
                dve.wait_ge(S["osq_done"], b + 1)
                nc.vector.reduce_sum(ons[:, 0, :], osq.rearrange("p (n d) -> p n d", d=DB), AX.X).then_inc(S["osum_done"], 1)
                dve.wait_ge(S["oroot_done"], b + 1)
                chained(nc.vector.tensor_scalar(ons[:, 1, :], ons[:, 1, :], col(SC), 1e-30, ALU.mult, ALU.max))
                chained(nc.vector.reciprocal(ons[:, 0, :], ons[:, 1, :]))
                chained(nc.vector.tensor_scalar(ons[:, 1, :], ons[:, 0, :], col(XMAX), 1.0, ALU.mult, ALU.min))
                o3 = o_all.rearrange("p (n d) -> p n d", d=DB)
                nc.vector.tensor_tensor(o3, o3, ons[:, 1, :].unsqueeze(2).to_broadcast([P, TB * HB, DB]), ALU.mult
                                        ).then_inc(S["o_scaled"], 1)
                for t in range(TB):
                    dve.wait_ge(S["out_done"], b * TB + t + 1)
                    dve.wait_ge(S["x_back"], (b + 1) * 64)
                    xt = env.X[:, bass.ds(b * TB + t, 1), :].rearrange("p a d -> p (a d)")
                    nc.vector.tensor_tensor(xt, bank(2 + t % 2, 0, D), xt, ALU.add).then_inc(S["x_added"], 1)
                while base[1] < FACTORS:
                    chained(nc.vector.tensor_copy(col(T + 10), col(ONE)))
                assert base[1] == FACTORS, base[1]
                dve.wait_ge(S["x_added"], (b + 1) * TB)

        @block.scalar
        def _(act):
            act.wait_ge(S["gz_done"], 1)
            T = 11
            nc.scalar.activation(col(T + 2, 2), col(T, 2), ACT.Exp).then_inc(S["scal"], 1)
            act.wait_ge(S["scal"], 1)
            nc.scalar.activation(col(T + 4, 2), col(T + 2, 2), ACT.Ln, bias=col(ONE)).then_inc(S["scal"], 1)
            act.wait_ge(S["gz_done"], 2)
            nc.scalar.activation(col(SC), col(C), ACT.Sqrt).then_inc(S["scal"], 1)
            act.wait_ge(S["gz_done"], 3)
            nc.scalar.activation(col(T + 9), col(T + 7), ACT.Ln).then_inc(S["scal"], 1)
            with act.Fori(0, BATCH) as b:
                act.wait_ge(S["x_added"], b * TB)
                for q in range(TB // 4 + 1):
                    if q < TB // 4:
                        act.wait_ge(S["xT_done"], b * TB + 4 * q + 4)
                        for c in range(KC):
                            nc.scalar.activation(xnT[:, c, q * BANK:(q + 1) * BANK], bank(4 + c), ACT.Copy
                                                 ).then_inc(S["xT_copied"], 1)
                    for t in range(max(4 * q - 4, 0), 4 * q):
                        act.wait_ge(S["proj_done"], b * TB + t + 1)
                        ps = half_ps(t % 2)[:, 0:3 * D]
                        if t >= 2:
                            act.wait_ge(S["nsq_done"], b * TB + t - 1)
                        nc.scalar.activation(sq[:, t % 2, :], ps, ACT.Square).then_inc(S["sq_done"], 1)
                        nc.scalar.activation(tok[:, :, t, :], ps.rearrange("p (a n) -> p a n", a=3), ACT.Copy
                                             ).then_inc(S["tok_copied"], 1)
                act.wait_ge(S["nsq_done"], (b + 1) * TB)
                nc.scalar.activation(tmp[:, 0:3, :], nsq, ACT.Sqrt).then_inc(S["root_all"], 1)
                act.wait_ge(S["x_all"], b + 1)
                nc.scalar.activation(tmp[:, 3:5, :], tmp[:, 0:2, :], ACT.Tanh).then_inc(S["th_all"], 1)
                act.wait_ge(S["raT_done"], b + 1)
                nc.scalar.activation(raT, bank(6, 0, 2 * P).rearrange("p (c k) -> p c k", c=2), ACT.Copy
                                     ).then_inc(S["raT_copied"], 1)

                def square(g, k):
                    if SQUARES[k] != "A":
                        return
                    act.wait_ge(S["a_ready"], g * NCHK + k + 1)
                    act.wait_ge(S["av_done"], g * NCHK + k + 1)
                    nc.scalar.activation(y_slot(k), a_ring[:, slot(A_RING, k), :], ACT.Square).then_inc(S["sq_A"], 1)

                def root(g, k):
                    act.wait_ge(S["sq_" + SQUARES[k]], squared(g, k) + 1)
                    nc.scalar.activation(y_slot(k), y_slot(k), ACT.Sqrt, bias=col(MINUS1)).then_inc(S["root_done"], 1)

                def log(g, k):
                    act.wait_ge(S["sum_done"], summed(g * NCHK + k + 1))
                    nc.scalar.activation(y_slot(k), y_slot(k), ACT.Ln).then_inc(S["ln_done"], 1)

                def weight(g, k):
                    act.wait_ge(S["ln_done"], g * NCHK + k + 1)
                    nc.scalar.activation(y_slot(k), y_slot(k), ACT.Exp, bias=col(SHIFT), scale=col(NEG_S)
                                         ).then_inc(S["w_done"], 1)

                def batch(first, second, g, n):
                    ks = range(n * BATCHED, (n + 1) * BATCHED)
                    for k in ks:
                        first(g, k)
                        if k > ks[0]:
                            second(g, k - 1)
                    second(g, ks[-1])

                def roots(g, n):
                    batch(square, root, g, n)

                def weights(g, n):
                    nc.scalar.preload_act_table_set("natural_log_exp_and_others")
                    batch(log, weight, g, n)

                NB = NCHK // BATCHED
                act.wait_ge(S["x_saved"], (b + 1) * 64)
                roots(b * HB, 0)
                with act.Fori(0, HB - 1) as h:
                    for n in range(NB):
                        roots(b * HB + h + (n + 1) // NB, (n + 1) % NB)
                        weights(b * HB + h, n)
                for n in range(NB):
                    if n + 1 < NB:
                        roots(b * HB + HB - 1, n + 1)
                    weights(b * HB + HB - 1, n)
                g = b * HB + HB
                act.wait_ge(S["osum_done"], b + 1)
                nc.scalar.activation(ons[:, 1, :], ons[:, 0, :], ACT.Sqrt).then_inc(S["oroot_done"], 1)
                for t in range(TB):
                    act.wait_ge(S["loT_done"], b * TB + t + 1)
                    if t >= 2:
                        act.wait_ge(S["out_done"], b * TB + t - 1)
                    nc.scalar.activation(oT[:, t % 2, :], bank(t % 2, 0, D), ACT.Copy).then_inc(S["loT_copied"], 1)

        @block.tensor
        def _(pe):
            pe.sem_inc(S["av_done"], Y_RING)
            with pe.Fori(0, BATCH) as b:
                for q in range(TB // 4 + 1):
                    pe.wait_ge(S["xT_copied"], (b * (TB // 4) + q) * KC)
                    for t in range(4 * q, 4 * q + 4 if q < TB // 4 else 0):
                        pe.wait_ge(S["xn_done"], b * TB + t + 1)
                        for c in range(KC):
                            last = nc.tensor.transpose(bank(4 + c, t % 4 * P, (t % 4 + 1) * P),
                                                       xn[:, t % 4, c * P:(c + 1) * P], env.ident[:, :])
                        last.then_inc(S["xT_done"], 1)
                    if q == 0:
                        pe.wait_ge(S["w_loaded"], (b + 1) * 16)
                        continue
                    for t in range(4 * q - 4, 4 * q):
                        if t >= 2:
                            pe.wait_ge(S["tok_copied"], b * TB + t - 1)
                        for a, z in ((0, BANK), (BANK, 3 * D)):
                            for c in range(KC):
                                last = nc.tensor.matmul(half_ps(t % 2)[:, a:z], xnT[:, c, t * P:(t + 1) * P],
                                                        w_in[:, c, a:z], start=(c == 0), stop=(c == KC - 1))
                        last.then_inc(S["proj_done"], 1)
                pe.wait_ge(S["ra_done"], b + 1)
                for c in range(2):
                    last = nc.tensor.transpose(bank(6, c * P, (c + 1) * P), ons[:, 2, c * P:(c + 1) * P], env.ident[:, :])
                last.then_inc(S["raT_done"], 1)
                pe.wait_ge(S["tok_copied"], (b + 1) * TB)
                pe.wait_ge(S["raT_copied"], b + 1)

                def group(g, i, j):
                    if i == 0:
                        pe.wait_ge(S["stack_done"], g + 1)
                    pe.wait_ge(S["grp_copied"], g * 4 + max(i - 1, 0))
                    ps = bank(6 + (i + 1) % 2).bitcast(BF16)
                    for t in range(8):
                        src = stack[:, i // 2, (i % 2) * 8 + t, :, :].rearrange("p s d -> p (s d)")
                        last = nc.tensor.transpose(ps[0:KST, t * P:(t + 1) * P], src, env.ident_bf[:, :])
                    last.then_inc(S["grpT_done"], 1)

                def scores(g, k, j, first):
                    for s in range(2):
                        n = g * 2 * NCHK + 2 * k + s
                        if first and k == 0:
                            pe.wait_ge(S["scores_read"], g * 2 * NCHK)
                        elif k > 0:
                            pe.wait_ge(S["scores_read"], n - 1)
                        else:
                            pe.wait_ge(S["scores_read"], g * 2 * NCHK - (1 - s))
                        for i in range(2):
                            cs = slice(s * HALF + i * BANK, s * HALF + (i + 1) * BANK)
                            last = nc.tensor.matmul(half_ps(s)[:, i * BANK:(i + 1) * BANK], kT[:, j, k * P:(k + 1) * P],
                                                    qT[:, j, cs], start=True, stop=True)
                        last.then_inc(S["scores_done"], 1)

                def product(g, k, j):
                    pe.wait_ge(S["w_done"], g * NCHK + k + 1)
                    if k == 0:
                        pe.wait_ge(S["v_ready"], g + 1)
                        pe.wait_ge(S["o_copied"], g_before(g))
                    for i in range(4):
                        last = nc.tensor.matmul(bank(4 + j)[32 * i:32 * i + 32, :], v_aug[:, j, k, :],
                                                y_slot(k)[:, i * BANK:(i + 1) * BANK],
                                                start=(k == 0), stop=(k == NCHK - 1), skip_group_check=True)
                    last.then_inc(S["av_done"], 1)

                def products_after(k):
                    return {BATCHED - 2: [k - 10], BATCHED - 1: [k - 10, k - 9, k - 8]}.get(k % BATCHED, [])

                def g_before(g):
                    return g_first[0] if g_first[0] is not None else g - 1

                g_first = [None]

                def out_transposes(g):
                    pe.wait_ge(S["o_copied"], g + 1)
                    for c in range(4):
                        last = nc.tensor.transpose(bank(6, c * P, (c + 1) * P), o_sb[:, c * P:(c + 1) * P], env.ident[:, :])
                    last.then_inc(S["oT_done"], 1)

                for i in range(4):
                    group(b * HB, i, 0)
                pe.wait_ge(S["grp_copied"], b * HB * 4 + 4)

                def head(h, j, first, last):
                    g = b * HB + h
                    for k in range(NCHK):
                        scores(g, k, j, first)
                        for m in products_after(k):
                            if m >= 0:
                                g_first[0] = b * HB if first else None
                                product(g, m, j)
                                g_first[0] = None
                            elif not first:
                                product(g - 1, m + NCHK, 1 - j)
                        if not first and k == 10:
                            out_transposes(g - 1)
                        if not last and 11 <= k < 15:
                            if k == 12:
                                pe.wait_ge(S["o_done"], g * 4)
                                pe.wait_ge(S["scores_read"], g * 2 * NCHK)
                            group(g + 1, k - 11, 1 - j)
                    if not last:
                        pe.wait_ge(S["grp_copied"], (g + 2) * 4)
                        pe.sem_inc(S["passed"], 1)

                head(0, 0, True, False)
                with pe.Fori(0, HB // 2 - 1) as i:
                    head(i * 2 + 1, 1, False, False)
                    head(i * 2 + 2, 0, False, False)
                head(HB - 1, 1, False, True)
                g = b * HB + HB
                for k in range(NCHK - Y_RING, NCHK):
                    product(g - 1, k, 1)
                out_transposes(g - 1)
                pe.wait_ge(S["o_scaled"], b + 1)
                pe.wait_ge(S["wo_loaded"], (b + 1) * 16)
                def transpose_out(t):
                    if t >= 2:
                        pe.wait_ge(S["loT_copied"], b * TB + t - 1)
                    for c in range(KC):
                        last = nc.tensor.transpose(bank(t % 2, c * P, (c + 1) * P), tok[:, 0, t, c * P:(c + 1) * P],
                                                   env.ident[:, :])
                    last.then_inc(S["loT_done"], 1)

                transpose_out(0)
                for t in range(TB):
                    if t + 1 < TB:
                        transpose_out(t + 1)
                    pe.wait_ge(S["loT_copied"], b * TB + t + 1)
                    if t >= 2:
                        pe.wait_ge(S["x_added"], b * TB + t - 1)
                    for c in range(KC):
                        last = nc.tensor.matmul(bank(2 + t % 2, 0, D), oT[:, t % 2, c * P:(c + 1) * P], wo_sb[:, c, :],
                                                start=(c == 0), stop=(c == KC - 1))
                    last.then_inc(S["out_done"], 1)
                pe.wait_ge(S["x_added"], (b + 1) * TB)


def program(nc, x, wqk, wv, wo, bo, slopes, w_cat, right_aug, w_qkv, w_o, scalars, out):
    ra_scratch = nc.dram_tensor("ra_scratch", (BATCH, TB * HB, P), F32).ap()
    x_scratch = nc.dram_tensor("x_scratch", (BATCH * SEQ, D), F32).ap()
    with ExitStack() as ctx:
        env = make_env(nc, ctx)
        stage_load(nc, env, x)
        stage_ln_stats(nc, env, "ln0")
        stage_attn_a(nc, env, wqk, wv, wo, bo, slopes)
        stage_ln_stats(nc, env, "ln1")
        stage_ffn(nc, env, "ffn0", w_cat, right_aug)
        stage_ln_stats(nc, env, "ln2")
        stage_attn_b(nc, env, w_qkv, w_o, scalars, ra_scratch, x_scratch)
        stage_ln_stats(nc, env, "ln3")
        stage_ffn(nc, env, "ffn1", w_cat, right_aug, out=out)


def kernel(**inputs):
    import numpy as np
    import concourse.bacc as _bacc
    from concourse.bass_utils import run_bass_kernel_spmd as _run

    i = {k[3:]: np.asarray(v) for k, v in inputs.items()}
    wqk = np.stack([i[n].reshape(KC, P, HA, DH).transpose(2, 1, 0, 3) for n in ("attn_a_Wq", "attn_a_Wk")], 2)
    base = np.float32((2.0 ** 8) ** (1.0 / HA))
    slopes = (np.float32(1.0) / base ** np.arange(1, HA + 1, dtype=np.float32)).reshape(1, HA)
    arrays = {
        "x": i["attn_a_x"].reshape(BATCH * SEQ, D),
        "wqk": wqk,
        "wv": i["attn_a_Wv"].reshape(KC, P, PAIRS, 2 * DH).transpose(2, 1, 0, 3),
        "wo": i["attn_a_Wo"].reshape(PAIRS, 2 * DH, D),
        "bo": i["attn_a_bo"].reshape(1, D),
        "slopes": slopes,
        "w_cat": np.concatenate([i["ffn_W_lin"].T, i["ffn_gate_w"].T, i["ffn_left"].transpose(1, 0, 2).reshape(D, E * R)], 1),
        "right_aug": np.concatenate([i["ffn_right"].reshape(E * R, D), i["ffn_b_lin"].reshape(1, D)], 0),
        "w_qkv": np.concatenate([i["attn_b_W_q"].T, i["attn_b_W_k"].T, i["attn_b_W_v"].T], 1),
        "w_o": i["attn_b_W_o"].T,
        "scalars": np.stack([i["attn_b_log_c"], i["attn_b_beta"]]).reshape(1, 2),
    }
    nc = _bacc.Bacc("TRN2", target_bir_lowering=False, num_devices=1)
    fed, args = {}, {}
    for name, a in arrays.items():
        a = np.ascontiguousarray(a)
        fed[f"in_{name}_dram"] = a
        args[name] = nc.dram_tensor(f"in_{name}_dram", a.shape, F32, kind="ExternalInput").ap()
    args["out"] = nc.dram_tensor("out_0_dram", (BATCH * SEQ, D), F32, kind="ExternalOutput").ap()
    program(nc, **args)
    r = _run(nc, [fed], core_ids=[0])
    return r.results[0]["out_0_dram"].reshape(BATCH, SEQ, D)
```
